# Optimizing a Trainium2 kernel written in Bass

```python
import numpy as np
import jax
import jax.numpy as jnp

def _softmax(x, axis=-1):
    return jax.nn.softmax(x, axis=axis)

def _gelu(x):
    return jax.nn.gelu(x, approximate=True)

def _silu(x):
    return jax.nn.silu(x)

def _sigmoid(x):
    return jax.nn.sigmoid(x)

def _layernorm(x, axis=-1, eps=1e-05):
    m = jnp.mean(x, axis=axis, keepdims=True)
    v = jnp.var(x, axis=axis, keepdims=True)
    return (x - m) / jnp.sqrt(v + eps)

def _scatter_add(tgt, idx, src, axis=0):
    return tgt.at[idx].add(src)

def _segment_sum(src, seg, n):
    return jax.ops.segment_sum(src, seg, n)
kernel_name = 'mk_decoder_preln_d1_seqx_r4_095a4c'

def setup_inputs(seed: int=0):
    np.random.seed(seed)
    _w = jnp.asarray

    def _rec_inputs():
        import jax
        import jax.numpy as jnp
        _rk = jax.random.key(seed)
        x = 7.22e-05 + 1 * jax.random.normal(jax.random.fold_in(_rk, 1), (4, 1024, 256), jnp.float32)
        _lenS = 1024 - jax.random.randint(jax.random.fold_in(_rk, 7), (4,), 0, max(1, 1024 // 4) + 1, jnp.int32)
        _lenS2 = 77 - jax.random.randint(jax.random.fold_in(_rk, 8), (4,), 0, max(1, 77 // 4) + 1, jnp.int32)
        _ctx_1024P = jax.random.normal(jax.random.fold_in(_rk, 11), (4, 16, 256), jnp.float32)
        _ctx_1024c = jax.random.dirichlet(jax.random.fold_in(_rk, 511), 0.3 * jnp.ones((16,), jnp.float32), (4, 77))
        _ctx_1024t = jnp.einsum('bsk,bkd->bsd', _ctx_1024c, _ctx_1024P)
        _ctx_1024t = _ctx_1024t * jax.lax.rsqrt(jnp.mean(jnp.square(_ctx_1024t)) + 1e-12) * 0.953939
        ctx_1024 = 4.13588e-05 + 0.999923 * (_ctx_1024t + 0.3 * jax.random.normal(jax.random.fold_in(_rk, 611), (4, 77, 256), jnp.float32))
        return (x, ctx_1024)
    x, ctx_1024 = _rec_inputs()

    def _L0_attn_setup():
        import jax, jax.numpy as jnp
        import numpy as np
        D_MODEL = 256
        N_HEADS = 16
        D_HEAD = D_MODEL // N_HEADS
        M_SLOPE = 0.5
        BATCH = 2
        SEQ = 512

        def _alibi_bias(n_heads, seq_len, m, dtype):
            slopes = m ** jnp.arange(n_heads, dtype=dtype)
            pos = jnp.arange(seq_len, dtype=dtype)
            dist = jnp.abs(pos[:, None] - pos[None, :])
            return -dist[None, :, :] * slopes[:, None, None]
        key = jax.random.key(seed)
        k1, k2, k3 = jax.random.split(key, 3)
        x = jax.random.normal(k1, (BATCH, SEQ, D_MODEL), dtype=jnp.float32)
        qkv_w = jax.random.normal(k2, (3 * D_MODEL, D_MODEL), dtype=jnp.float32) * (1.0 / np.sqrt(D_MODEL))
        qkv_b = jnp.zeros((3 * D_MODEL,), dtype=jnp.float32)
        out_w = jax.random.normal(k3, (D_MODEL, D_MODEL), dtype=jnp.float32) * (1.0 / np.sqrt(D_MODEL))
        out_b = jnp.zeros((D_MODEL,), dtype=jnp.float32)
        return {'x': x, 'qkv_w': qkv_w, 'qkv_b': qkv_b, 'out_w': out_w, 'out_b': out_b}
    _L0_attn_all = _L0_attn_setup()
    _L0_attn_in = {k: v for k, v in _L0_attn_all.items() if k in ('qkv_w', 'qkv_b', 'out_w', 'out_b')}
    del _L0_attn_all

    def _L0_xattn_setup():
        import jax, jax.numpy as jnp
        import numpy as np
        C = 256
        B, SQ, SKV = (4, 512, 512)
        key = jax.random.key(seed)
        ks = jax.random.split(key, 10)
        s = 1.0 / np.sqrt(C)
        return {'x': jax.random.normal(ks[0], (B, SQ, C), jnp.float32), 'content_embeddings': jax.random.normal(ks[1], (B, SKV, C), jnp.float32), 'Wq': jax.random.normal(ks[2], (C, C), jnp.float32) * s, 'bq': jnp.zeros((C,), jnp.float32), 'Wk': jax.random.normal(ks[3], (C, C), jnp.float32) * s, 'bk': jnp.zeros((C,), jnp.float32), 'Wv': jax.random.normal(ks[4], (C, C), jnp.float32) * s, 'bv': jnp.zeros((C,), jnp.float32), 'Wo': jax.random.normal(ks[5], (C, C), jnp.float32) * s, 'bo': jnp.zeros((C,), jnp.float32)}
    _L0_xattn_all = _L0_xattn_setup()
    _L0_xattn_in = {k: v for k, v in _L0_xattn_all.items() if k in ('Wq', 'bq', 'Wk', 'bk', 'Wv', 'bv', 'Wo', 'bo')}
    del _L0_xattn_all

    def _L0_ffn_setup():
        import jax, jax.numpy as jnp
        import numpy as np
        N_EMBD = 256
        NUM_EXPERTS = 8
        TOP_K = 2
        D_FF = 4 * N_EMBD
        B, S = (4, 512)
        key = jax.random.key(seed)
        ks = jax.random.split(key, 7)
        scale = lambda fan_in: 1.0 / np.sqrt(fan_in)
        x = jax.random.normal(ks[0], (B, S, N_EMBD), dtype=jnp.float32)
        W_router = jax.random.normal(ks[1], (N_EMBD, NUM_EXPERTS), dtype=jnp.float32) * scale(N_EMBD)
        b_router = jnp.zeros((NUM_EXPERTS,), dtype=jnp.float32)
        W1 = jax.random.normal(ks[2], (NUM_EXPERTS, N_EMBD, D_FF), dtype=jnp.float32) * scale(N_EMBD)
        b1 = jnp.zeros((NUM_EXPERTS, D_FF), dtype=jnp.float32)
        W2 = jax.random.normal(ks[3], (NUM_EXPERTS, D_FF, N_EMBD), dtype=jnp.float32) * scale(D_FF)
        b2 = jnpp = jnp.zeros((NUM_EXPERTS, N_EMBD), dtype=jnp.float32)
        return {'x': x, 'W_router': W_router, 'b_router': b_router, 'W1': W1, 'b1': b1, 'W2': W2, 'b2': b2}
    _L0_ffn_all = _L0_ffn_setup()
    _L0_ffn_in = {k: v for k, v in _L0_ffn_all.items() if k in ('W_router', 'b_router', 'W1', 'b1', 'W2', 'b2')}
    del _L0_ffn_all
    return {'x': x, 'ctx_1024': ctx_1024, 'L0_attn_qkv_w': _L0_attn_in['qkv_w'], 'L0_attn_qkv_b': _L0_attn_in['qkv_b'], 'L0_attn_out_w': _L0_attn_in['out_w'], 'L0_attn_out_b': _L0_attn_in['out_b'], 'L0_xattn_Wq': _L0_xattn_in['Wq'], 'L0_xattn_bq': _L0_xattn_in['bq'], 'L0_xattn_Wk': _L0_xattn_in['Wk'], 'L0_xattn_bk': _L0_xattn_in['bk'], 'L0_xattn_Wv': _L0_xattn_in['Wv'], 'L0_xattn_bv': _L0_xattn_in['bv'], 'L0_xattn_Wo': _L0_xattn_in['Wo'], 'L0_xattn_bo': _L0_xattn_in['bo'], 'L0_ffn_W_router': _L0_ffn_in['W_router'], 'L0_ffn_b_router': _L0_ffn_in['b_router'], 'L0_ffn_W1': _L0_ffn_in['W1'], 'L0_ffn_b1': _L0_ffn_in['b1'], 'L0_ffn_W2': _L0_ffn_in['W2'], 'L0_ffn_b2': _L0_ffn_in['b2']}

def reference(x, ctx_1024, L0_attn_qkv_w, L0_attn_qkv_b, L0_attn_out_w, L0_attn_out_b, L0_xattn_Wq, L0_xattn_bq, L0_xattn_Wk, L0_xattn_bk, L0_xattn_Wv, L0_xattn_bv, L0_xattn_Wo, L0_xattn_bo, L0_ffn_W_router, L0_ffn_b_router, L0_ffn_W1, L0_ffn_b1, L0_ffn_W2, L0_ffn_b2):
    import jax
    import jax.numpy as jnp

    def _L0_attn_ref(x, qkv_w, qkv_b, out_w, out_b):
        import jax, jax.numpy as jnp
        import numpy as np
        D_MODEL = 256
        N_HEADS = 16
        D_HEAD = D_MODEL // N_HEADS
        M_SLOPE = 0.5
        BATCH = 2
        SEQ = 512

        def _alibi_bias(n_heads, seq_len, m, dtype):
            slopes = m ** jnp.arange(n_heads, dtype=dtype)
            pos = jnp.arange(seq_len, dtype=dtype)
            dist = jnp.abs(pos[:, None] - pos[None, :])
            return -dist[None, :, :] * slopes[:, None, None]
        batch, seq_len, d_model = x.shape
        qkv = x @ qkv_w.T + qkv_b
        qkv = qkv.reshape(batch, seq_len, N_HEADS, 3 * D_HEAD).transpose(0, 2, 1, 3)
        q, k, v = jnp.split(qkv, 3, axis=-1)
        scale = jnp.sqrt(jnp.asarray(D_HEAD, dtype=x.dtype))
        scores = jnp.einsum('bhid,bhjd->bhij', q, k) / scale
        scores = scores + _alibi_bias(N_HEADS, seq_len, M_SLOPE, x.dtype)[None]
        attn = jax.nn.softmax(scores, axis=-1)
        out = jnp.einsum('bhij,bhjd->bhid', attn, v)
        out = out.transpose(0, 2, 1, 3).reshape(batch, seq_len, d_model)
        return out @ out_w.T + out_b

    def _L0_xattn_ref(x, content_embeddings, Wq, bq, Wk, bk, Wv, bv, Wo, bo):
        import jax, jax.numpy as jnp
        import numpy as np
        C = 256
        B, SQ, SKV = (4, 512, 512)
        queries = x @ Wq.T + bq
        keys = content_embeddings @ Wk.T + bk
        values = content_embeddings @ Wv.T + bv
        scale = 1.0 / jnp.sqrt(jnp.asarray(C, x.dtype))
        scores = jnp.einsum('bqc,bkc->bqk', queries, keys) * scale
        attn = jax.nn.softmax(scores, axis=-1)
        attended = jnp.einsum('bqk,bkc->bqc', attn, values)
        out = x + attended
        return out @ Wo.T + bo

    def _L0_ffn_ref(x, W_router, b_router, W1, b1, W2, b2):
        import jax, jax.numpy as jnp
        import numpy as np
        N_EMBD = 256
        NUM_EXPERTS = 8
        TOP_K = 2
        D_FF = 4 * N_EMBD
        B, S = (4, 512)
        Bv, Sv, D = x.shape
        flat_x = x.reshape(-1, D)
        T = flat_x.shape[0]
        logits = flat_x @ W_router + b_router
        top_vals, top_idx = jax.lax.top_k(logits, TOP_K)
        neg_inf = jnp.full_like(logits, -jnp.inf)
        sparse_logits = neg_inf.at[jnp.arange(T)[:, None], top_idx].set(top_vals)
        router_weights = jax.nn.softmax(sparse_logits, axis=-1)
        final_output = jnp.zeros_like(flat_x)
        for e in range(NUM_EXPERTS):
            expert_mask = jnp.any(top_idx == e, axis=-1)
            h = jax.nn.relu(flat_x @ W1[e] + b1[e])
            y = h @ W2[e] + b2[e]
            w = router_weights[:, e] * expert_mask.astype(x.dtype)
            final_output = final_output + y * w[:, None]
        return final_output.reshape(Bv, Sv, D)
    x = x + _L0_attn_ref(_layernorm(x, axis=-1), L0_attn_qkv_w, L0_attn_qkv_b, L0_attn_out_w, L0_attn_out_b)
    x = x + _L0_xattn_ref(_layernorm(x, axis=-1), ctx_1024, L0_xattn_Wq, L0_xattn_bq, L0_xattn_Wk, L0_xattn_bk, L0_xattn_Wv, L0_xattn_bv, L0_xattn_Wo, L0_xattn_bo)
    x = x + _L0_ffn_ref(_layernorm(x, axis=-1), L0_ffn_W_router, L0_ffn_b_router, L0_ffn_W1, L0_ffn_b1, L0_ffn_W2, L0_ffn_b2)
    return x

_drawn_inputs = setup_inputs


def setup_inputs(seed=0):
    import zlib

    import numpy as np

    out = dict(_drawn_inputs(seed))
    spreads = {'L0_attn_qkv_b': (0.0, 0.1),
     'L0_attn_out_b': (0.0, 0.1),
     'L0_xattn_bq': (0.0, 0.267),
     'L0_xattn_bk': (0.0, 0.8),
     'L0_xattn_bv': (0.0, 0.1),
     'L0_xattn_bo': (0.0, 0.1),
     'L0_ffn_b_router': (0.0, 0.1),
     'L0_ffn_b1': (0.0, 0.1),
     'L0_ffn_b2': (0.0, 0.1)}
    factors = {}
    for name, (base, spread) in spreads.items():
        noise = np.random.default_rng([zlib.crc32(name.encode()), seed]).standard_normal(out[name].shape)
        drawn = base * np.exp(spread * noise) if base else spread * noise
        out[name] = jnp.asarray(drawn.astype(out[name].dtype))
    for name, factor in factors.items():
        out[name] = (out[name] * factor).astype(out[name].dtype)
    return out
```

```python
import numpy as np
import concourse.bass as bass
from concourse import mybir

F32 = mybir.dt.float32
F32R = mybir.dt.float32r
F16 = mybir.dt.float16
I32 = mybir.dt.int32
U32 = mybir.dt.uint32
ALU = mybir.AluOpType
ACT = mybir.ActivationFunctionType
AX = mybir.AxisListType

P = 128
NB, S, D = 4, 1024, 256
NH, DH = 16, 16
CTX = 77
NE, FF = 8, 1024
TOPK = 2
EPS = 1e-5
NT = S // P
DC = D // P
FC = FF // P
BANK = 512
NCH = S // BANK
HG = 4
NG = NH // HG
HROWS = 64
TOK = NB * S
NTT = TOK // P
NBLK = (TOK * TOPK) // P + NE - 1
NSLOT = NBLK * P
VW = DH + 1


class Program:

    def __init__(self, nc, ctx):
        self.nc, self.ctx = nc, ctx
        self.queues = {e: [] for e in ("tensor", "vector", "scalar", "gpsimd", "sync")}
        self.sems, self.counts, self.waited = {}, {}, {}

    def do(self, engine, step, signal=None, by=1):
        sem = None
        if signal is not None:
            if signal not in self.sems:
                self.sems[signal] = self.ctx.enter_context(self.nc.semaphore(signal))
                self.counts[signal] = 0
            sem = self.sems[signal]
            self.counts[signal] += by
        self.queues[engine].append((step, sem, by))
        return (signal, self.counts[signal]) if signal is not None else None

    def sign(self, engine, signal):
        step, sem, _ = self.queues[engine].pop()
        assert sem is None
        return self.do(engine, step, signal)

    def mark(self, signal):
        return signal, self.counts[signal]

    def wait(self, engine, *marks):
        for mark in marks:
            if mark is None:
                continue
            name, count = mark
            if self.waited.get((engine, name), 0) >= count:
                continue
            self.waited[engine, name] = count
            sem = self.sems[name]
            self.queues[engine].append((lambda e, s=sem, c=count: e.wait_ge(s, c), None, 0))

    def play(self, engine, e):
        for step, sem, by in self.queues[engine]:
            ins = step(e)
            if sem is not None:
                ins.then_inc(sem, by)


def build(nc, t):
    from contextlib import ExitStack
    with ExitStack() as ctx:
        prog = Program(nc, ctx)
        do, wait = prog.do, prog.wait
        ps = ctx.enter_context(nc.psum_tensor("ps", [P, 8, BANK], F32))
        last_read = [None] * 8

        def sb(stack, name, shape, dt=F32):
            return stack.enter_context(nc.sbuf_tensor(name, shape, dt))

        def dma(step, signal, engine="sync"):
            return do(engine, step, signal, 16)

        def pe_into(banks, *marks):
            wait("tensor", *[last_read[b] for b in banks], *marks)

        def read_by(banks, mark):
            for b in banks:
                last_read[b] = mark

        x2_dram = nc.dram_tensor("x2_scratch", [TOK, D], F32, kind="Internal").ap()
        yn_dram = nc.dram_tensor("yn_scratch", [TOK, D], F32, kind="Internal").ap()
        xs_dram = nc.dram_tensor("slot_in", [NSLOT, D], F32, kind="Internal").ap()
        ys_dram = nc.dram_tensor("slot_out", [NSLOT, D], F32, kind="Internal").ap()

        ident = sb(ctx, "ident", [P, P])
        logits = sb(ctx, "logits", [P, NTT, NE])
        zero_rows = sb(ctx, "zero_rows", [P, 4 * D])
        const_in = dma(lambda e: e.dma_start(ident[:, :], t["c_ident"]), "consts_in")
        zeroed = do("vector", lambda e: e.memset(zero_rows[:, :], 0.0), "dve_setup")
        wait("sync", zeroed)
        xs_zero = None
        per = 4
        for n in range(0, NBLK, per):
            k = min(per, NBLK - n)
            xs_zero = dma(lambda e, n=n, k=k: e.dma_start(
                xs_dram[n * P:(n + k) * P, :].rearrange("(p r) d -> p (r d)", p=P),
                zero_rows[:, 0:k * D]), "slots_zeroed")

        attn = ExitStack()
        with attn:
            attention_parts(nc, t, prog, attn, sb, dma, pe_into, read_by, ps, ident, logits,
                            x2_dram, yn_dram, const_in)
        moe = ExitStack()
        with moe:
            expert_parts(nc, t, prog, moe, sb, dma, pe_into, read_by, ps, ident, logits,
                         x2_dram, yn_dram, xs_dram, ys_dram, xs_zero)

        block = ctx.enter_context(nc.Block())

        @block.sync
        def _(e):
            prog.play("sync", e)

        @block.scalar
        def _(e):
            prog.play("scalar", e)

        @block.vector
        def _(e):
            prog.play("vector", e)

        @block.gpsimd
        def _(e):
            prog.play("gpsimd", e)

        @block.tensor
        def _(e):
            prog.play("tensor", e)


def attention_parts(nc, t, prog, stack, sb_, dma, pe_into, read_by, ps, ident, logits,
                    x2_dram, yn_dram, const_in):
    do, wait = prog.do, prog.wait
    sb = lambda name, shape, dt=F32: sb_(stack, name, shape, dt)

    wqkv = sb("wqkv", [P, DC, 3 * D])
    bqk = sb("bqk", [P, 2, DC])
    bqk4 = sb("bqk4", [P, 2, DC])
    bv_all = sb("bv_all", [P, D])
    wo = sb("wo", [P, DC, D])
    bo_all = sb("bo_all", [P, D])
    xwo = sb("xwo", [P, DC, D])
    xbo_all = sb("xbo_all", [P, D])
    wr = sb("wr", [P, DC, NE])
    br_all = sb("br_all", [P, NE])
    slopes = sb("slopes", [P, NH, P], F16)
    ramps = sb("ramps", [P, 2, BANK], F16)
    kspec = sb("kspec", [P, 2, S], F32R)
    qspec = sb("qspec", [DH, S], F32R)
    ones_row = sb("ones_row", [1, P])
    minus_half = sb("minus_half", [P, NT])
    ctx_keys = sb("ctx_keys", [P, NB, DC, CTX])
    ctx_vals = sb("ctx_vals", [CTX, NB, D])
    ctx_bias = sb("ctx_bias", [1, NB, CTX])

    loads = [
        (wqkv[:, :, :], t["wqkv"].rearrange("(c p) n -> p c n", p=P)),
        (bqk[:, :, :], t["bqk"]),
        (bv_all[:, :], t["bv"].broadcast_to([P, D])),
        (wo[:, :, :], t["wo"].rearrange("(c p) n -> p c n", p=P)),
        (bo_all[:, :], t["bo"].broadcast_to([P, D])),
        (xwo[:, :, :], t["xwo"].rearrange("(c p) n -> p c n", p=P)),
        (xbo_all[:, :], t["xbo"].broadcast_to([P, D])),
        (wr[:, :, :], t["wr"].rearrange("(c p) n -> p c n", p=P)),
        (br_all[:, :], t["br"].broadcast_to([P, NE])),
    ]
    for dst, src in loads:
        weights_in = dma(lambda e, dst=dst, src=src: e.dma_start(dst, src), "consts_in")

    do("vector", lambda e: e.memset(ones_row[:, :], 1.0), "dve_setup")
    halves = do("vector", lambda e: e.memset(minus_half[:, :], -0.5), "dve_setup")

    with ExitStackOf() as pre:
        cst = sb_(pre, "cst", [P, 2, S])
        slo = sb_(pre, "slo", [P, NH])
        rmp = sb_(pre, "rmp", [P, 2, BANK])
        qsp = sb_(pre, "qsp", [DH, S])
        dma(lambda e: e.dma_start(cst[:, :, :], t["c_kspec"].rearrange("(a p) n -> p a n", p=P)), "consts_in")
        dma(lambda e: e.dma_start(slo[:, :], t["c_slopes"].broadcast_to([P, NH])), "consts_in")
        dma(lambda e: e.dma_start(rmp[:, :, :], t["c_ramps"].rearrange("a p n -> p a n")), "consts_in")
        dma(lambda e: e.dma_start(qsp[:, :], t["c_qspec"]), "consts_in")
        xw = {}
        for n in ("wq", "wk", "wv"):
            xw[n] = sb_(pre, "x" + n, [P, DC, D])
            dma(lambda e, n=n: e.dma_start(xw[n][:, :, :], t["x" + n].rearrange("(c p) n -> p c n", p=P)), "consts_in")
        xbq = sb_(pre, "xbq", [P, DC])
        xbk = sb_(pre, "xbk", [P, DC])
        xbv = sb_(pre, "xbv", [P, DC])
        for b_, n in ((xbq, "xbq"), (xbk, "xbk"), (xbv, "xbv")):
            dma(lambda e, b_=b_, n=n: e.dma_start(b_[:, :], t[n]), "consts_in")
        cx = sb_(pre, "cx", [P, NB, D])
        all_in = dma(lambda e: e.dma_start(cx[0:CTX, :, :], t["ctx"].rearrange("b c d -> c b d")), "consts_in")

        wait("vector", all_in)
        do("vector", lambda e: e.tensor_copy(kspec[:, :, :], cst[:, :, :]), "dve_setup")
        do("vector", lambda e: e.tensor_copy(qspec[:, :], qsp[:, :]), "dve_setup")
        do("vector", lambda e: e.tensor_copy(ramps[:, :, :], rmp[:, :, :]), "dve_setup")
        for h in range(NH):
            do("vector", lambda e, h=h: e.tensor_scalar(slopes[:, h, :], ident[:, :], slo[:, h:h + 1], None, ALU.mult), "dve_setup")
        do("vector", lambda e: e.tensor_scalar(bqk4[:, 0, :], bqk[:, 0, :], DH ** -0.5, None, ALU.mult), "dve_setup")
        setup = do("vector", lambda e: e.tensor_copy(bqk4[:, 1, :], bqk[:, 1, :]), "dve_setup")

        cT = sb_(pre, "cT", [P, DC, NB, CTX])
        kT = sb_(pre, "kT", [P, DC, NB, CTX])
        vT = sb_(pre, "vT", [P, DC, NB, CTX])
        NC = NB * CTX
        wait("tensor", all_in)
        for c in range(DC):
            for b in range(NB):
                m = do("tensor", lambda e, b=b, c=c: e.transpose(
                    ps[:, c, b * CTX:(b + 1) * CTX], cx[0:CTX, b, c * P:(c + 1) * P], ident[0:CTX, 0:CTX]), "pe_setup")
        wait("vector", m)
        for c in range(DC):
            m = do("vector", lambda e, c=c: e.tensor_copy(cT[:, c, :, :].rearrange("p b j -> p (b j)"), ps[:, c, 0:NC]), "dve_setup")
        wait("tensor", m)
        for i, (w, out_, bias) in enumerate(((xw["wk"], kT, xbk), (xw["wv"], vT, xbv))):
            for mo in range(DC):
                for c in range(DC):
                    m = do("tensor", lambda e, w=w, mo=mo, c=c, i=i: e.matmul(
                        ps[:, 2 + 2 * i + mo, 0:NC], w[:, c, mo * P:(mo + 1) * P],
                        cT[:, c, :, :].rearrange("p b j -> p (b j)"), start=(c == 0), stop=(c == DC - 1)), "pe_setup")
                wait("vector", m)
                m = do("vector", lambda e, out_=out_, mo=mo, i=i, bias=bias: e.tensor_scalar(
                    out_[:, mo, :, :].rearrange("p b j -> p (b j)"), ps[:, 2 + 2 * i + mo, 0:NC],
                    bias[:, mo:mo + 1], None, ALU.add), "dve_setup")
        wait("tensor", m)
        for mo in range(DC):
            for c in range(DC):
                m = do("tensor", lambda e, mo=mo, c=c: e.matmul(
                    ps[:, mo, 0:NC], xw["wq"][:, c, mo * P:(mo + 1) * P],
                    kT[:, c, :, :].rearrange("p b j -> p (b j)"), start=(c == 0), stop=(c == DC - 1)), "pe_setup")
            wait("vector", m)
            do("vector", lambda e, mo=mo: e.tensor_copy(
                ctx_keys[:, :, mo, :], ps[:, mo, 0:NC].rearrange("p (b j) -> p b j", b=NB)), "dve_setup")
        for c in range(DC):
            m = do("tensor", lambda e, c=c: e.matmul(
                ps[0:1, 6, 0:NC], xbq[:, c:c + 1], kT[:, c, :, :].rearrange("p b j -> p (b j)"),
                start=(c == 0), stop=(c == DC - 1)), "pe_setup")
        wait("vector", m)
        do("vector", lambda e: e.tensor_copy(ctx_bias[:, :, :].rearrange("p b j -> p (b j)"), ps[0:1, 6, 0:NC]), "dve_setup")
        vals_out = {}
        for b in range(NB):
            bank = 7 if b % 2 else 5
            if b >= 2:
                wait("tensor", vals_out[b - 2])
            for c in range(DC):
                m = do("tensor", lambda e, b=b, c=c, bank=bank: e.matmul(
                    ps[0:CTX, bank, 0:D], vT[:, c, b, :], xwo[:, c, :], start=(c == 0), stop=(c == DC - 1)), "pe_setup")
            wait("vector", m)
            vals_out[b] = setup = do("vector", lambda e, b=b, bank=bank: e.tensor_copy(ctx_vals[:, b, :], ps[0:CTX, bank, 0:D]), "dve_setup")
        read_by(range(8), setup)

    x = [sb(f"x{i}", [P, NT, D]) for i in range(2)]
    xn = sb("xn", [P, NT, D])
    xT = sb("xT", [P, DC, S])
    stats = sb("stats", [P, NT, 6])
    mv = sb("mv", [P, NT, 2])
    vep = sb("vep", [P, NT])
    rstd = sb("rstd", [P, NT])
    full = sb("full", [P, 2, BANK])
    hi = [sb(f"hi{a}", [P, DC, S], F32R) for a in "qk"]
    lo = [sb(f"lo{a}", [P, DC, S], F32R) for a in "qk"]
    qa = [sb(f"qa{i}", [P, HG // 2, S], F32R) for i in range(2)]
    ka = [sb(f"ka{i}", [P, HG, S], F32R) for i in range(2)]
    vt = sb("vt", [P, NT, NH, VW])
    NP = 4
    prob = sb("prob", [P, NP, 2, BANK])
    av = [sb(f"av{i}", [P, BANK]) for i in range(2)]
    on = sb("on", [P, NT, D])
    rden = sb("rden", [P, HG])
    rmax = sb("rmax", [P, HG, NT])
    nmax = sb("nmax", [P, HG * NT])
    nrow = sb("nrow", [HG * NT, P], F32R)
    sc = sb("sc", [P, NT, CTX])
    smax = sb("smax", [P, NT])
    ssum = sb("ssum", [P, NT])
    pT = sb("pT", [CTX, S])

    for i in range(2):
        for h in range(HG):
            r = HROWS * (1 - h % 2)
            setup = do("vector", lambda e, i=i, h=h, r=r: e.memset(ka[i][r:r + HROWS, h, :].bitcast(F32), 0.0), "dve_setup")
    setup = do("vector", lambda e: e.memset(vt[:, :, :, DH:VW], 1.0), "dve_setup")
    for i in range(2):
        setup = do("vector", lambda e, i=i: e.memset(av[i][:, :], 0.0), "dve_setup")

    def transposed(src, banks, src_ready):
        pe_into(banks, src_ready)
        for c in range(DC):
            for tt in range(NT):
                b = banks[(c * NT + tt) // 4]
                off = (tt % 4) * P
                m = do("tensor", lambda e, c=c, tt=tt, b=b, off=off: e.transpose(
                    ps[:, b, off:off + P], src[:, tt, c * P:(c + 1) * P], ident[:, :]), "pe_turn")
            eng = "scalar" if c == 0 else "vector"
            wait(eng, m)
            b0 = banks[c * 2]
            src_ps = ps[:, b0:b0 + 2, :].rearrange("p b n -> p (b n)")
            if eng == "scalar":
                m0 = do(eng, lambda e, c=c, s=src_ps: e.activation(xT[:, c, :], s, ACT.Copy), "act_turned")
                read_by(banks[0:2], m0)
            else:
                m1 = do(eng, lambda e, c=c, s=src_ps: e.tensor_copy(xT[:, c, :], s), "dve_turned")
                read_by(banks[2:4], m1)
        return m0, m1

    def layer_norm(src, ready):
        wait("vector", *ready)
        for tt in range(NT):
            m = do("vector", lambda e, tt=tt: e.bn_stats(stats[:, tt, :], src[:, tt, :]), "dve_norm")
        wait("vector", m)
        for tt in range(NT):
            m = do("vector", lambda e, tt=tt: e.bn_aggr(mv[:, tt, :], stats[:, tt, :]), "dve_norm")
        wait("vector", m)
        m = do("vector", lambda e: e.tensor_scalar(vep[:, :], mv[:, :, 1], EPS, None, ALU.add), "dve_norm")
        wait("gpsimd", m)
        m = do("gpsimd", lambda e: e.tensor_tensor(rstd[:, :], vep[:, :], minus_half[:, :], ALU.pow), "pool_rstd")
        wait("vector", m)
        for tt in range(NT):
            m = do("vector", lambda e, tt=tt: e.tensor_scalar(
                xn[:, tt, :], src[:, tt, :], mv[:, tt, 0:1], rstd[:, tt:tt + 1], ALU.subtract, ALU.mult), "dve_norm")
        return m

    state = {"unit": 0, "av_free": [None, None], "group_done": [None, None], "xT_free": None,
             "xn_free": None, "spread": [None, None], "prob_free": [None] * NP, "ka_special": None}

    def load_x(b):
        return dma(lambda e: e.dma_start(x[b % 2][:, :, :], t["x"][b].rearrange("(t p) d -> p t d", p=P)),
                   f"x_in{b % 2}")

    wait("sync", setup)
    x_ready = {0: load_x(0), 1: load_x(1)}
    x_stored = {}

    def batch(b):
        xb = x[b % 2]
        wait("vector", setup, state["xn_free"])
        xn_done = layer_norm(xb, [x_ready[b]])
        wait("gpsimd", xn_done, weights_in, x_ready[b])
        for tt in range(NT):
            xbo_done = do("gpsimd", lambda e, tt=tt: e.tensor_tensor(xb[:, tt, :], xb[:, tt, :], bo_all[:, :], ALU.add), "pool_bias")
        wait("tensor", setup)
        wait("scalar", state["xT_free"])
        wait("vector", state["xT_free"])
        turned = transposed(xn, [0, 1, 2, 3], xn_done)
        wait("tensor", *turned)
        wait("vector", *state["spread"])
        wait("scalar", *state["spread"])
        split_done = None
        full_free = [None, None]
        n = 0
        for a in range(2):
            for mo in range(DC):
                for ch in range(NCH):
                    bank = 4 + n % 4
                    slot = n % 2
                    pe_into([bank])
                    for c in range(DC):
                        m = do("tensor", lambda e, a=a, mo=mo, ch=ch, c=c, bank=bank: e.matmul(
                            ps[:, bank, :], wqkv[:, c, a * D + mo * P:a * D + (mo + 1) * P],
                            xT[:, c, ch * BANK:(ch + 1) * BANK], start=(c == 0), stop=(c == DC - 1)), "pe_proj")
                    cols = slice(ch * BANK, (ch + 1) * BANK)
                    wait("scalar", m, full_free[slot])
                    mf = do("scalar", lambda e, a=a, mo=mo, bank=bank, slot=slot: e.activation(
                        full[:, slot, :], ps[:, bank, :], ACT.Identity, bias=bqk4[:, a, mo:mo + 1],
                        scale=(DH ** -0.5 if a == 0 else 1.0)), "act_full")
                    read_by([bank], mf)
                    wait("vector", mf)
                    mh = do("vector", lambda e, a=a, mo=mo, cols=cols, slot=slot: e.tensor_copy(
                        hi[a][:, mo, cols], full[:, slot, :]), "dve_split")
                    wait("vector", mh)
                    full_free[slot] = split_done = do("vector", lambda e, a=a, mo=mo, cols=cols, slot=slot: e.tensor_tensor(
                        lo[a][:, mo, cols], full[:, slot, :], hi[a][:, mo, cols].bitcast(F32), ALU.subtract), "dve_split")
                    n += 1
        for tt in range(NT):
            bank = tt % 4
            pe_into([bank])
            for c in range(DC):
                m = do("tensor", lambda e, tt=tt, c=c, bank=bank: e.matmul(
                    ps[:, bank, 0:D], xT[:, c, tt * P:(tt + 1) * P], wqkv[:, c, 2 * D:3 * D],
                    start=(c == 0), stop=(c == DC - 1)), "pe_proj")
            wait("vector", m)
            v_done = do("vector", lambda e, tt=tt, bank=bank: e.tensor_tensor(
                vt[:, tt, :, 0:DH], ps[:, bank, 0:D].rearrange("p (h d) -> p h d", h=NH),
                bv_all[:, :].rearrange("p (h d) -> p h d", h=NH), ALU.add), "dve_v")
            read_by([bank], v_done)
        state["xT_free"] = state["xn_free"] = m

        def spread(g):
            i = (b * NG + g) % 2
            wait("sync", split_done, state["group_done"][i], setup)
            for hh in range(HG):
                h = g * HG + hh
                mo, r = h // 8, (h % 8) * DH
                base = HROWS * (hh % 2)
                for j, part in enumerate((qspec[:, :], hi[0][r:r + DH, mo, :], lo[0][r:r + DH, mo, :], hi[0][r:r + DH, mo, :])):
                    dma(lambda e, i=i, hh=hh, base=base, j=j, part=part: e.dma_start(
                        qa[i][base + DH * j:base + DH * (j + 1), hh // 2, :].bitcast(F32), part.bitcast(F32)), f"spread{i}")
                for j, part in enumerate((kspec[r:r + DH, mo, :], hi[1][r:r + DH, mo, :], hi[1][r:r + DH, mo, :], lo[1][r:r + DH, mo, :])):
                    m = dma(lambda e, i=i, hh=hh, base=base, j=j, part=part: e.dma_start(
                        ka[i][base + DH * j:base + DH * (j + 1), hh, :].bitcast(F32), part.bitcast(F32)), f"spread{i}")
            state["spread"][i] = m
            return m

        spread_done = {0: spread(0), 1: spread(1)}
        def group(g):
            i = (b * NG + g) % 2
            wait("tensor", spread_done[g])
            for hh in range(HG):
                h = g * HG + hh
                for qt in range(NT):
                    pair = ((hh * NT + qt) % 3) * 2
                    pe_into([pair, pair + 1])
                    for kc in range(NCH):
                        do("tensor", lambda e, i=i, hh=hh, qt=qt, kc=kc, pair=pair: e.matmul(
                            ps[:, pair + kc, :], qa[i][:, hh // 2, qt * P:(qt + 1) * P],
                            ka[i][:, hh, kc * BANK:(kc + 1) * BANK], start=True, stop=True))
                        if qt // 4 == kc:
                            r_ = qt % 4
                            cols, pat = ((slice(P * r_, BANK), ramps[:, 1, 0:BANK - P * r_]) if kc == 0 else
                                         (slice(0, P * (r_ + 1)), ramps[:, 0, BANK - P * (r_ + 1):BANK]))
                            do("tensor", lambda e, h=h, pair=pair, kc=kc, cols=cols, pat=pat: e.matmul(
                                ps[:, pair + kc, cols], slopes[:, h, :], pat, start=False, stop=True,
                                skip_group_check=True))
                    m = prog.sign("tensor", "pe_max")
                    wait("vector", m)
                    mm_ = do("vector", lambda e, hh=hh, qt=qt, pair=pair: e.tensor_reduce(
                        rmax[:, hh, qt:qt + 1], ps[:, pair:pair + 2, :].rearrange("p a n -> p (a n)"), AX.X, ALU.max), "dve_max")
                    read_by([pair, pair + 1], mm_)
            wait("vector", mm_)
            m = do("vector", lambda e: e.tensor_scalar(nmax[:, :], rmax[:, :, :].rearrange("p a n -> p (a n)"), -1.0, None, ALU.mult), "dve_max")
            pe_into([6], m)
            m = do("tensor", lambda e: e.transpose(ps[0:HG * NT, 6, 0:P], nmax[:, :], ident[:, :]), "pe_max")
            wait("vector", m, state.get("nrow_free"))
            m = do("vector", lambda e: e.tensor_copy(nrow[:, :], ps[0:HG * NT, 6, 0:P]), "dve_max")
            read_by([6], m)
            wait("sync", m)
            for hh in range(HG):
                base = HROWS * (hh % 2)
                m = dma(lambda e, i=i, hh=hh, base=base: e.dma_start(
                    qa[i][base + 2:base + 3, hh // 2, :].bitcast(F32),
                    nrow[hh * NT:(hh + 1) * NT, :].bitcast(F32)), "max_rows")
            state["nrow_free"] = m
            wait("tensor", m)

            def scores(ch, kt, pair_n):
                u = state["unit"]
                pair = (u % 3) * 2
                pe_into([pair, pair + 1])
                for k in range(2):
                    hh = pair_n * 2 + k
                    h = g * HG + hh
                    do("tensor", lambda e, i=i, hh=hh, kt=kt, ch=ch, k=k, pair=pair: e.matmul(
                        ps[:, pair + k, :], ka[i][:, hh, kt * P:(kt + 1) * P],
                        qa[i][:, hh // 2, ch * BANK:(ch + 1) * BANK], start=True, stop=True))
                    if kt // 4 == ch:
                        r_ = kt % 4
                        cols, pat = ((slice(0, P * (r_ + 1)), ramps[:, 0, BANK - P * (r_ + 1):BANK]) if kt < 4 else
                                     (slice(P * r_, BANK), ramps[:, 1, 0:BANK - P * r_]))
                        do("tensor", lambda e, h=h, pair=pair, k=k, cols=cols, pat=pat: e.matmul(
                            ps[:, pair + k, cols], slopes[:, h, :], pat, start=False, stop=True,
                            skip_group_check=True))
                m = prog.sign("tensor", "pe_scores")
                slot = u % NP
                wait("scalar", m, state["prob_free"][slot])
                m = do("scalar", lambda e, slot=slot, pair=pair: e.activation(
                    prob[:, slot, :, :], ps[:, pair:pair + 2, :], ACT.Exp), "act_prob")
                read_by([pair, pair + 1], m)
                state["unit"] += 1
                return slot, m

            def attend(ch, kt, made):
                bank = 6 + ch
                if kt == 0:
                    pe_into([bank])
                for pn, (slot, m) in enumerate(made):
                    wait("tensor", m)
                    for k in range(2):
                        hh = pn * 2 + k
                        h = g * HG + hh
                        do("tensor", lambda e, kt=kt, h=h, hh=hh, slot=slot, k=k, bank=bank: e.matmul(
                            ps[32 * hh:32 * hh + VW, bank, :], vt[:, kt, h, :], prob[:, slot, k, :],
                            start=(kt == 0), stop=(kt == NT - 1)))
                    m = prog.sign("tensor", "pe_attend")
                    state["prob_free"][slot] = m
                return m

            def finish(ch, m):
                bank = 6 + ch
                a = av[ch]
                wait("vector", m, state["av_free"][ch])
                for hh in range(HG):
                    m = do("vector", lambda e, hh=hh, bank=bank, a=a: e.tensor_copy(
                        a[32 * hh:32 * hh + VW, :], ps[32 * hh:32 * hh + VW, bank, :]), "dve_av")
                read_by([bank], m)
                pe_into([bank], m)
                for q in range(4):
                    m = do("tensor", lambda e, q=q, bank=bank, a=a: e.transpose(
                        ps[:, bank, q * P:(q + 1) * P], a[:, q * P:(q + 1) * P], ident[:, :]), "pe_av")
                state["av_free"][ch] = m
                wait("vector", m)
                for q in range(4):
                    tile_ = ps[:, bank, q * P:(q + 1) * P].rearrange("p (h c) -> p h c", h=HG)
                    tt = ch * 4 + q
                    wait("vector", state.get("rden_free"))
                    mr = do("vector", lambda e, tile_=tile_: e.reciprocal(rden[:, :], tile_[:, :, DH]), "dve_on")
                    wait("vector", mr)
                    m = do("vector", lambda e, tile_=tile_, tt=tt: e.tensor_tensor(
                        on[:, tt, g * HG * DH:(g + 1) * HG * DH].rearrange("p (h d) -> p h d", h=HG),
                        tile_[:, :, 0:DH], rden[:, :].unsqueeze(2).broadcast_to([P, HG, DH]), ALU.mult), "dve_on")
                    state["rden_free"] = m
                read_by([bank], m)
                return m

            wait("tensor", v_done)
            if g == 0:
                wait("vector", state.get("on_free"))
            for ch in range(NCH):
                pend = []
                last = None
                for kt in range(NT):
                    pend.append((kt, [scores(ch, kt, 0), scores(ch, kt, 1)]))
                    if len(pend) > 1:
                        kk, made = pend.pop(0)
                        last = attend(ch, kk, made)
                kk, made = pend.pop(0)
                last = attend(ch, kk, made)
                if ch == NCH - 1:
                    state["group_done"][i] = last
                    if g + 2 < NG:
                        spread_done[g + 2] = spread(g + 2)
                on_done = finish(ch, last)
            return on_done

        for g in range(NG):
            on_done = group(g)

        wait("scalar", state["xT_free"])
        turned = transposed(on, [0, 1, 2, 3], on_done)
        state["on_free"] = prog.mark("pe_turn")
        wait("tensor", *turned)
        wait("vector", xbo_done)
        for tt in range(NT):
            bank = 4 + tt % 4
            pe_into([bank])
            for c in range(DC):
                m = do("tensor", lambda e, tt=tt, c=c, bank=bank: e.matmul(
                    ps[:, bank, 0:D], xT[:, c, tt * P:(tt + 1) * P], wo[:, c, :], start=(c == 0), stop=(c == DC - 1)), "pe_proj")
            wait("vector", m)
            x1_done = do("vector", lambda e, tt=tt, bank=bank: e.tensor_tensor(
                xb[:, tt, :], ps[:, bank, 0:D], xb[:, tt, :], ALU.add), "dve_x1")
            read_by([bank], x1_done)
        state["xT_free"] = m
        xn_done = layer_norm(xb, [x1_done, state["xn_free"]])
        wait("gpsimd", xn_done, x1_done)
        for tt in range(NT):
            xbo_done = do("gpsimd", lambda e, tt=tt: e.tensor_tensor(xb[:, tt, :], xb[:, tt, :], xbo_all[:, :], ALU.add), "pool_bias")
        wait("scalar", state["xT_free"])
        wait("vector", state["xT_free"])
        turned = transposed(xn, [0, 1, 2, 3], xn_done)
        wait("tensor", *turned)
        for tt in range(NT):
            bank, off = 4 + tt // 4, (tt % 4) * CTX
            if tt % 4 == 0:
                pe_into([bank])
            for c in range(DC):
                do("tensor", lambda e, tt=tt, c=c, bank=bank, off=off, b=b: e.matmul(
                    ps[:, bank, off:off + CTX], xT[:, c, tt * P:(tt + 1) * P], ctx_keys[:, b, c, :],
                    start=(c == 0), stop=False))
            m = do("tensor", lambda e, bank=bank, off=off, b=b: e.matmul(
                ps[:, bank, off:off + CTX], ones_row[:, :], ctx_bias[:, b, :], start=False, stop=True), "pe_proj")
        wait("vector", m, state.get("sc_free"))
        for k in range(2):
            view = ps[:, 4 + k, 0:4 * CTX].rearrange("p (t j) -> p t j", t=4)
            m = do("vector", lambda e, k=k, view=view: e.tensor_reduce(smax[:, 4 * k:4 * k + 4], view, AX.X, ALU.max), "dve_sm")
            wait("vector", m)
            m = do("vector", lambda e, k=k, view=view: e.tensor_tensor(
                sc[:, 4 * k:4 * k + 4, :], view, smax[:, 4 * k:4 * k + 4].unsqueeze(2).broadcast_to([P, 4, CTX]), ALU.subtract), "dve_sm")
            read_by([4 + k], m)
        wait("scalar", m)
        m = do("scalar", lambda e: e.activation(sc[:, :, :], sc[:, :, :], ACT.Exp, scale=D ** -0.5), "act_sm")
        wait("vector", m)
        m = do("vector", lambda e: e.tensor_reduce(ssum[:, :], sc[:, :, :], AX.X, ALU.add), "dve_sm")
        wait("vector", m)
        m = do("vector", lambda e: e.reciprocal(smax[:, :], ssum[:, :]), "dve_sm")
        wait("vector", m)
        m = do("vector", lambda e: e.tensor_tensor(sc[:, :, :], sc[:, :, :], smax[:, :].unsqueeze(2).broadcast_to([P, NT, CTX]), ALU.mult), "dve_sm")
        pe_into([0, 1], m)
        for tt in range(NT):
            m = do("tensor", lambda e, tt=tt: e.transpose(
                ps[0:CTX, tt // 4, (tt % 4) * P:(tt % 4 + 1) * P], sc[:, tt, :], ident[:, :]), "pe_turn")
        state["sc_free"] = m
        wait("scalar", m, state.get("pT_free"))
        m = do("scalar", lambda e: e.activation(pT[:, :], ps[0:CTX, 0:2, :].rearrange("p a n -> p (a n)"), ACT.Copy), "act_turned")
        read_by([0, 1], m)
        wait("tensor", m)
        wait("vector", xbo_done)
        for tt in range(NT):
            bank = 4 + tt % 4
            pe_into([bank])
            for c in range(DC):
                do("tensor", lambda e, tt=tt, c=c, bank=bank: e.matmul(
                    ps[:, bank, 0:D], xT[:, c, tt * P:(tt + 1) * P], xwo[:, c, :], start=(c == 0), stop=False))
            m = do("tensor", lambda e, tt=tt, bank=bank, b=b: e.matmul(
                ps[:, bank, 0:D], pT[:, tt * P:(tt + 1) * P], ctx_vals[:, b, :], start=False, stop=True), "pe_proj")
            wait("vector", m)
            x2_done = do("vector", lambda e, tt=tt, bank=bank: e.tensor_tensor(
                xb[:, tt, :], ps[:, bank, 0:D], xb[:, tt, :], ALU.add), "dve_x1")
            read_by([bank], x2_done)
        state["pT_free"] = state["xT_free"] = m
        wait("sync", x2_done)
        x_stored[b] = dma(lambda e, b=b, xb=xb: e.dma_start(
            x2_dram[b * S:(b + 1) * S, :].rearrange("(t p) d -> p t d", p=P), xb[:, :, :]), f"x2_out{b % 2}")
        xn_done = layer_norm(xb, [x2_done])
        if b + 2 < NB:
            wait("sync", x_stored[b], xn_done)
            x_ready[b + 2] = load_x(b + 2)
        wait("scalar", state["xT_free"])
        wait("vector", state["xT_free"])
        turned = transposed(xn, [0, 1, 2, 3], xn_done)
        wait("sync", xn_done)
        yn_done = dma(lambda e, b=b: e.dma_start(
            yn_dram[b * S:(b + 1) * S, :].rearrange("(t p) d -> p t d", p=P), xn[:, :, :]), "yn_out")
        wait("tensor", *turned)
        pe_into([7])
        for tt in range(NT):
            for c in range(DC):
                m = do("tensor", lambda e, tt=tt, c=c: e.matmul(
                    ps[:, 7, tt * NE:(tt + 1) * NE], xT[:, c, tt * P:(tt + 1) * P], wr[:, c, :],
                    start=(c == 0), stop=(c == DC - 1)), "pe_proj")
        state["xT_free"] = m
        state["xn_free"] = yn_done
        wait("vector", m)
        logits_done = do("vector", lambda e, b=b: e.tensor_tensor(
            logits[:, b * NT:(b + 1) * NT, :], ps[:, 7, 0:NT * NE].rearrange("p (t n) -> p t n", t=NT),
            br_all[:, :].unsqueeze(1).broadcast_to([P, NT, NE]), ALU.add), "dve_logits")
        read_by([7], logits_done)
        return logits_done, yn_done

    for b in range(NB):
        logits_done, yn_done = batch(b)
    prog.attention_end = [logits_done, yn_done, x_stored[NB - 2], x_stored[NB - 1],
                          state["group_done"][0], state["group_done"][1]]


def ExitStackOf():
    from contextlib import ExitStack
    return ExitStack()


def expert_parts(nc, t, prog, stack, sb_, dma, pe_into, read_by, ps, ident, logits,
                 x2_dram, yn_dram, xs_dram, ys_dram, xs_zero):
    do, wait = prog.do, prog.wait
    sb = lambda name, shape, dt=F32: sb_(stack, name, shape, dt)
    free_again = prog.attention_end

    w1 = sb("w1", [P, NE, DC, FF])
    w2 = sb("w2", [P, NE, FC, D])
    b1_all = sb("b1_all", [P, NE, FF])
    b2_all = sb("b2_all", [P, NE, D])
    slot = [sb(f"slot{k}", [P, NTT], I32) for k in range(TOPK)]
    weight = [sb(f"weight{k}", [P, NTT]) for k in range(TOPK)]
    expert_of = sb("expert_of", [P, P], I32)

    wait("sync", *free_again)
    for n in range(NE):
        dma(lambda e, n=n: e.dma_start(w1[:, n, :, :], t["w1"][n].rearrange("(c p) f -> p c f", p=P)), "experts_in")
    dma(lambda e: e.dma_start(b1_all[:, :, :].rearrange("p n f -> p (n f)"), t["b1"].rearrange("n f -> (n f)").unsqueeze(0).broadcast_to([P, NE * FF])), "experts_in")
    for n in range(NE):
        dma(lambda e, n=n: e.dma_start(w2[:, n, :, :], t["w2"][n].rearrange("(c p) f -> p c f", p=P)), "experts_in")
    experts_in = dma(lambda e: e.dma_start(b2_all[:, :, :].rearrange("p n f -> p (n f)"), t["b2"].rearrange("n f -> (n f)").unsqueeze(0).broadcast_to([P, NE * D])), "experts_in")

    with ExitStackOf() as rt:
        r = lambda name, shape, dt=F32: sb_(rt, name, shape, dt)
        earlier = r("earlier", [P, P])
        every = r("every", [P, P])
        steps = r("steps", [P, P])
        ramp8 = r("ramp8", [P, NE])
        ones32 = r("ones32", [P, NTT])
        chosen = [r(f"chosen{k}", [P, NTT, NE]) for k in range(TOPK)]
        rest = r("rest", [P, NTT, NE])
        tmp = r("tmp", [P, NTT, NE])
        top = [r(f"top{k}", [P, NTT]) for k in range(TOPK)]
        first = r("first", [P, NTT])
        mask = r("mask", [P, NTT, NE])
        place = r("place", [P, NTT, NE])
        upto = r("upto", [P, NTT, NE])
        blocks_gt = r("blocks_gt", [P, NE, NTT])
        nblocks = r("nblocks", [P, NE])
        end = r("end", [P, NE])
        base = r("base", [P, NE])
        past = r("past", [P, NBLK, NE])
        ebf = r("ebf", [P, NBLK])
        slotf = r("slotf", [P, NTT])
        wt = r("wt", [P, NTT])
        ynb = [r(f"ynb{i}", [P, NT, D]) for i in range(2)]

        dma(lambda e: e.dma_start(earlier[:, :], t["c_low"]), "route_in")
        route_in = dma(lambda e: e.dma_start(steps[:, :], t["c_first"]), "route_in")
        wait("vector", *free_again, route_in)
        dve = [None]

        def v(step):
            wait("vector", dve[0])
            dve[0] = do("vector", step, "dve_route")
            return dve[0]

        bc = lambda a: a.unsqueeze(2).broadcast_to([P, NTT, NE])
        be = lambda a: a.unsqueeze(1).broadcast_to([P, NTT, NE])
        v(lambda e: e.memset(every[:, :], 1.0))
        v(lambda e: e.memset(ones32[:, :], 1.0))
        v(lambda e: e.tensor_scalar(ramp8[:, :], steps[:, 0:NE], -1.0 / P, float(NE), ALU.mult, ALU.add))
        src = logits
        for k in range(TOPK):
            v(lambda e, k=k, src=src: e.tensor_reduce(top[k][:, :], src[:, :, :], AX.X, ALU.max))
            v(lambda e, k=k, src=src: e.tensor_tensor(tmp[:, :, :], src[:, :, :], bc(top[k][:, :]), ALU.is_equal))
            v(lambda e: e.tensor_tensor(tmp[:, :, :], tmp[:, :, :], be(ramp8[:, :]), ALU.mult))
            v(lambda e: e.tensor_reduce(first[:, :], tmp[:, :, :], AX.X, ALU.max))
            v(lambda e, k=k: e.tensor_tensor(chosen[k][:, :, :], bc(first[:, :]), be(ramp8[:, :]), ALU.is_equal))
            if k == 0:
                v(lambda e: e.scalar_tensor_tensor(out=rest[:, :, :].rearrange("p t n -> p (t n)"),
                                                   in0=chosen[0][:, :, :].rearrange("p t n -> p (t n)"), scalar=-3.0e38,
                                                   in1=logits[:, :, :].rearrange("p t n -> p (t n)"), op0=ALU.mult, op1=ALU.add))
            src = rest
        m = v(lambda e: e.tensor_tensor(wt[:, :], top[1][:, :], top[0][:, :], ALU.subtract))
        wait("scalar", m)
        m = do("scalar", lambda e: e.activation(wt[:, :], wt[:, :], ACT.Exp), "act_route")
        wait("vector", m)
        v(lambda e: e.tensor_scalar(first[:, :], wt[:, :], 1.0, None, ALU.add))
        v(lambda e: e.reciprocal(weight[0][:, :], first[:, :]))
        v(lambda e: e.tensor_tensor(weight[1][:, :], weight[0][:, :], wt[:, :], ALU.mult))
        m = v(lambda e: e.tensor_tensor(mask[:, :, :], chosen[0][:, :, :], chosen[1][:, :, :], ALU.add))
        pe_into([0, 1], m)
        do("tensor", lambda e: e.matmul(ps[:, 0, 0:NTT * NE], earlier[:, :], mask[:, :, :].rearrange("p t n -> p (t n)"), start=True, stop=True))
        m = do("tensor", lambda e: e.matmul(ps[:, 1, 0:NTT * NE], every[:, :], mask[:, :, :].rearrange("p t n -> p (t n)"), start=True, stop=True), "pe_route")
        wait("vector", m)
        v(lambda e: e.tensor_copy(tmp[:, :, :], ps[:, 1, 0:NTT * NE].rearrange("p (t n) -> p t n", n=NE)))
        for n in range(NE):
            v(lambda e, n=n: e.tensor_tensor_scan(upto[:, :, n], ones32[:, :], tmp[:, :, n], 0.0, ALU.mult, ALU.add))
        v(lambda e: e.tensor_tensor(place[:, :, :], upto[:, :, :], tmp[:, :, :], ALU.subtract))
        m = v(lambda e: e.tensor_tensor(place[:, :, :], ps[:, 0, 0:NTT * NE].rearrange("p (t n) -> p t n", n=NE), place[:, :, :], ALU.add))
        read_by([0, 1], m)
        v(lambda e: e.tensor_tensor(blocks_gt[:, :, :], upto[:, NTT - 1, :].unsqueeze(2).broadcast_to([P, NE, NTT]),
                                    steps[:, 0:NTT].unsqueeze(1).broadcast_to([P, NE, NTT]), ALU.is_gt))
        v(lambda e: e.tensor_reduce(nblocks[:, :], blocks_gt[:, :, :], AX.X, ALU.add))
        v(lambda e: e.tensor_tensor_scan(end[:, :], ones32[:, 0:NE], nblocks[:, :], 0.0, ALU.mult, ALU.add))
        v(lambda e: e.tensor_tensor(base[:, :], end[:, :], nblocks[:, :], ALU.subtract))
        v(lambda e: e.tensor_scalar(base[:, :], base[:, :], float(P), None, ALU.mult))
        v(lambda e: e.tensor_tensor(place[:, :, :], place[:, :, :], be(base[:, :]), ALU.add))
        for k in range(TOPK):
            v(lambda e, k=k: e.tensor_tensor(tmp[:, :, :], place[:, :, :], chosen[k][:, :, :], ALU.mult))
            v(lambda e: e.tensor_reduce(slotf[:, :], tmp[:, :, :], AX.X, ALU.add))
            slots_done = v(lambda e, k=k: e.tensor_copy(slot[k][:, :], slotf[:, :]))
        v(lambda e: e.tensor_scalar(ebf[:, :], steps[:, 0:NBLK], 1.0 / P, None, ALU.mult))
        v(lambda e: e.tensor_tensor(past[:, :, :], ebf[:, :].unsqueeze(2).broadcast_to([P, NBLK, NE]),
                                    end[:, :].unsqueeze(1).broadcast_to([P, NBLK, NE]), ALU.is_ge))
        v(lambda e: e.tensor_reduce(ebf[:, :], past[:, :, :], AX.X, ALU.add))
        v(lambda e: e.tensor_scalar(ebf[:, :], ebf[:, :], float(NE - 1), None, ALU.min))
        experts_known = v(lambda e: e.tensor_copy(expert_of[:, 0:NBLK], ebf[:, :]))

        wait("gpsimd", *free_again, slots_done, xs_zero)
        scattered = [None, None]
        for b in range(NB):
            i = b % 2
            wait("scalar", *free_again, scattered[i])
            m = dma(lambda e, b=b, i=i: e.dma_start(ynb[i][:, :, :], yn_dram[b * S:(b + 1) * S, :].rearrange("(t p) d -> p t d", p=P)), f"yn_back{i}", "scalar")
            wait("gpsimd", m)
            for tt in range(NT):
                for k in range(TOPK):
                    scattered[i] = dma(lambda e, b=b, i=i, tt=tt, k=k: e.indirect_dma_start(
                        xs_dram, bass.IndirectOffsetOnAxis(ap=slot[k][:, b * NT + tt:b * NT + tt + 1], axis=0),
                        ynb[i][:, tt, :], None), f"scattered{i}", "gpsimd")

    NX = 3
    bk = ExitStackOf()
    sb = lambda name, shape, dt=F32: sb_(bk, name, shape, dt)
    xi = [sb(f"xi{i}", [P, D]) for i in range(NX)]
    xiT = [sb(f"xiT{i}", [P, DC, P]) for i in range(2)]
    hid = [sb(f"hid{i}", [P, FF]) for i in range(2)]
    hidT = [sb(f"hidT{i}", [P, FC, P]) for i in range(2)]
    yo = [sb(f"yo{i}", [P, D]) for i in range(2)]
    wait("sync", *scattered, experts_known)
    wait("tensor", experts_known, experts_in)
    wait("vector", *scattered, experts_in)
    wait("scalar", *scattered)
    turned, made, regs = {}, {}, {}
    rd = {}

    def load_block(n):
        wait("sync", rd.get(("xi", n - NX)))
        rd["in", n] = dma(lambda e, n=n: e.dma_start(xi[n % NX][:, :], xs_dram[n * P:(n + 1) * P, :]), f"slots_in{n % NX}")

    def turn_block(n):
        pe_into([0], rd["in", n])
        for c in range(DC):
            m = do("tensor", lambda e, n=n, c=c: e.transpose(ps[:, 0, c * P:(c + 1) * P], xi[n % NX][:, c * P:(c + 1) * P], ident[:, :]), "pe_x")
        rd["xi", n] = m
        wait("scalar", m, rd.get(("up", n - 2)))
        rd["xiT", n] = m = do("scalar", lambda e, n=n: e.activation(xiT[n % 2][:, :, :].rearrange("p c n -> p (c n)"), ps[:, 0, 0:D], ACT.Copy), "act_x")
        read_by([0], m)

    def up(n, half):
        bank = 1 + 2 * (n % 2) + half
        pe_into([bank], rd["xiT", n])
        if half == 0:
            do("tensor", lambda e, n=n: Load(e, regs, ("t", n), expert_of, n))
        for c in range(DC):
            m = do("tensor", lambda e, n=n, c=c, bank=bank, half=half: e.matmul(
                ps[:, bank, :], xiT[n % 2][:, c, :], w1[:, bass.ds(regs["t", n], 1), c, half * BANK:(half + 1) * BANK].rearrange("p a f -> p (a f)"),
                start=(c == 0), stop=(c == DC - 1)), "pe_up")
        rd["up", n] = m
        if half == 0:
            wait("vector", experts_known)
            do("vector", lambda e, n=n: Load(e, regs, ("v", n), expert_of, n))
        wait("vector", m, rd.get(("turn", n - 2)))
        rd["hid", n] = m = do("vector", lambda e, n=n, half=half, bank=bank: e.tensor_tensor(
            hid[n % 2][:, half * BANK:(half + 1) * BANK], ps[:, bank, :],
            b1_all[:, bass.ds(regs["v", n], 1), half * BANK:(half + 1) * BANK].rearrange("p a f -> p (a f)"), ALU.add), "dve_up")
        read_by([bank], m)

    def turn_hidden(n):
        pe_into([5, 6], rd["hid", n])
        for c in range(FC):
            m = do("tensor", lambda e, n=n, c=c: e.transpose(ps[:, 5 + c // 4, (c % 4) * P:(c % 4 + 1) * P], hid[n % 2][:, c * P:(c + 1) * P], ident[:, :]), "pe_h")
        rd["turn", n] = m
        wait("scalar", m, rd.get(("down", n - 2)))
        rd["hidT", n] = m = do("scalar", lambda e, n=n: e.activation(
            hidT[n % 2][:, :, :].rearrange("p c n -> p (c n)"), ps[:, 5:7, :].rearrange("p a n -> p (a n)"), ACT.Relu), "act_h")
        read_by([5, 6], m)

    def down(n):
        pe_into([7], rd["hidT", n])
        for c in range(FC):
            m = do("tensor", lambda e, n=n, c=c: e.matmul(
                ps[:, 7, 0:D], hidT[n % 2][:, c, :], w2[:, bass.ds(regs["t", n], 1), c, :].rearrange("p a f -> p (a f)"),
                start=(c == 0), stop=(c == FC - 1)), "pe_down")
        rd["down", n] = m
        wait("vector", m, rd.get(("out", n - 2)))
        m = do("vector", lambda e, n=n: e.tensor_tensor(
            yo[n % 2][:, :], ps[:, 7, 0:D], b2_all[:, bass.ds(regs["v", n], 1), :].rearrange("p a f -> p (a f)"), ALU.add), "dve_down")
        read_by([7], m)
        wait("sync", m)
        rd["out", n] = dma(lambda e, n=n: e.dma_start(ys_dram[n * P:(n + 1) * P, :], yo[n % 2][:, :]), f"slots_out{n % 2}")

    for n in range(min(NX, NBLK)):
        load_block(n)
    turn_block(0)
    up(0, 0)
    up(0, 1)
    turn_block(1)
    for n in range(NBLK):
        if n + 1 < NBLK:
            up(n + 1, 0)
        turn_hidden(n)
        if n + 1 < NBLK:
            up(n + 1, 1)
        if n + 2 < NBLK:
            turn_block(n + 2)
        if n + NX < NBLK:
            load_block(n + NX)
        down(n)

    bk.close()

    NO = 4
    sb = lambda name, shape, dt=F32: sb_(stack, name, shape, dt)
    got = [sb(f"got{i}", [P, TOPK, D]) for i in range(NO)]
    res = [sb(f"res{i}", [P, D]) for i in range(NO)]
    wait("gpsimd", rd["out", NBLK - 1], rd["out", NBLK - 2])
    wait("sync", rd["out", NBLK - 1], rd["out", NBLK - 2])
    for tt in range(NTT):
        i = tt % NO
        wait("gpsimd", rd.get(("sum", tt - NO)))
        for k in range(TOPK):
            mg = dma(lambda e, i=i, k=k, tt=tt: e.indirect_dma_start(
                got[i][:, k, :], None, ys_dram, bass.IndirectOffsetOnAxis(ap=slot[k][:, tt:tt + 1], axis=0)), f"gathered{i}", "gpsimd")
        wait("sync", rd.get(("outd", tt - NO)))
        ml = dma(lambda e, i=i, tt=tt: e.dma_start(res[i][:, :], x2_dram[tt * P:(tt + 1) * P, :]), f"x2_back{i}")
        wait("vector", mg, ml)
        for k in range(TOPK):
            m = do("vector", lambda e, i=i, k=k, tt=tt: e.scalar_tensor_tensor(
                out=res[i][:, :], in0=got[i][:, k, :], scalar=weight[k][:, tt:tt + 1], in1=res[i][:, :], op0=ALU.mult, op1=ALU.add), "dve_sum")
            if k == 0:
                wait("vector", m)
        rd["sum", tt] = m
        wait("scalar", m)
        rd["outd", tt] = dma(lambda e, i=i, tt=tt: e.dma_start(t["out"][tt * P:(tt + 1) * P, :], res[i][:, :]), f"result{i}", "scalar")
    for i in range(NO):
        wait("scalar", rd["outd", NTT - NO + i])


def Load(e, regs, key, table, n):
    regs[key] = e.value_load(table[0:1, n:n + 1], min_val=0, max_val=NE - 1)
    return None


def constants():
    slopes = 0.5 ** np.arange(NH)
    pos = np.arange(S)
    kspec = np.zeros((NH, DH, S), np.float32)
    sign = np.where(pos < S // 2, 1.0, -1.0)
    kspec[:, 0, :] = slopes[:, None] * (sign * pos)[None, :]
    kspec[:, 1, :] = -slopes[:, None] * sign[None, :]
    kspec[:, 2, :] = 1.0
    qspec = np.zeros((DH, S), np.float32)
    qspec[0], qspec[1] = 1.0, pos
    p, f = np.arange(P)[:, None], np.arange(BANK)[None, :]
    ramps = np.stack([-2.0 * np.maximum(0, p + BANK - P - f), -2.0 * np.maximum(0, f - p)]) / 16.0
    return {
        "c_ident": np.eye(P, dtype=np.float32),
        "c_kspec": kspec.reshape(NH * DH, S),
        "c_slopes": (16.0 * slopes).astype(np.float32)[None, :],
        "c_ramps": ramps.astype(np.float32),
        "c_qspec": qspec,
        "c_low": (np.arange(P)[:, None] < np.arange(P)[None, :]).astype(np.float32),
        "c_first": np.tile(np.arange(P, dtype=np.float32)[None, :] * P, (P, 1)),
    }


def kernel(**inputs):
    import concourse.bacc as bacc
    from concourse.bass_utils import run_bass_kernel_spmd

    a = {k: np.asarray(v) for k, v in inputs.items()}
    qkv = a["L0_attn_qkv_w"].reshape(NH, 3, DH, D).transpose(3, 1, 0, 2).reshape(D, 3 * D)
    qkv_b = a["L0_attn_qkv_b"].reshape(NH, 3, DH).transpose(1, 0, 2).reshape(3, D)
    row = lambda v: v.reshape(1, -1)
    col = lambda v: v.reshape(DC, P).T
    arrays = {
        "x": a["x"], "ctx": a["ctx_1024"],
        "wqkv": qkv, "bqk": qkv_b[0:2].reshape(2, DC, P).transpose(2, 0, 1), "bv": qkv_b[2:3],
        "wo": a["L0_attn_out_w"].T, "bo": row(a["L0_attn_out_b"]),
        "xwo": a["L0_xattn_Wo"].T, "xbo": row(a["L0_xattn_bo"]),
        "xwq": a["L0_xattn_Wq"], "xwk": a["L0_xattn_Wk"].T, "xwv": a["L0_xattn_Wv"].T,
        "xbq": col(a["L0_xattn_bq"]), "xbk": col(a["L0_xattn_bk"]), "xbv": col(a["L0_xattn_bv"]),
        "wr": a["L0_ffn_W_router"], "br": row(a["L0_ffn_b_router"]),
        "w1": a["L0_ffn_W1"], "b1": a["L0_ffn_b1"], "w2": a["L0_ffn_W2"], "b2": a["L0_ffn_b2"],
        **constants(),
    }
    arrays = {k: np.ascontiguousarray(v) for k, v in arrays.items()}
    nc = bacc.Bacc("TRN2", target_bir_lowering=False, num_devices=1)
    t = {k: nc.dram_tensor("in_" + k, v.shape, mybir.dt.from_np(v.dtype), kind="ExternalInput").ap()
         for k, v in arrays.items()}
    t["out"] = nc.dram_tensor("out", [TOK, D], F32, kind="ExternalOutput").ap()
    build(nc, t)
    r = run_bass_kernel_spmd(nc, [{"in_" + k: v for k, v in arrays.items()}], core_ids=[0])
    return r.results[0]["out"].reshape(NB, S, D)
```

```python
from contextlib import ExitStack

import numpy as np
import concourse.bass as bass
from concourse import mybir

F32 = mybir.dt.float32
F32R = mybir.dt.float32r
F16 = mybir.dt.float16
I32 = mybir.dt.int32
U32 = mybir.dt.uint32
ALU = mybir.AluOpType
ACT = mybir.ActivationFunctionType
AX = mybir.AxisListType

P = 128
NB, S, D = 4, 1024, 256
NH, DH = 16, 16
CTX = 77
NE, FF = 8, 1024
TOPK = 2
EPS = 1e-5
NT = S // P
DC = D // P
FC = FF // P
BANK = 512
NCH = S // BANK
HG = 4
NG = NH // HG
HROWS = 64
TOK = NB * S
NTT = TOK // P
NBLK = (TOK * TOPK) // P + NE - 1
REGION = TOK + P
NIDLE = NE - 1
NROW = NE * REGION + NIDLE * P
VW = DH + 1
CT = 32
NSET = 3
NPROB = 3
MAXIMA = (1, 1, 1, 1, 1)


class Program:

    def __init__(self, nc, ctx):
        self.nc, self.ctx = nc, ctx
        self.queues = {e: [] for e in ("tensor", "vector", "scalar", "gpsimd", "sync")}
        self.sems, self.counts, self.waited = {}, {}, {}

    def do(self, engine, step, signal=None, by=1):
        sem = None
        if signal is not None:
            if signal not in self.sems:
                self.sems[signal] = self.ctx.enter_context(self.nc.semaphore(signal))
                self.counts[signal] = 0
            sem = self.sems[signal]
            self.counts[signal] += by
        self.queues[engine].append((step, sem, by))
        return (signal, self.counts[signal]) if signal is not None else None

    def sign(self, engine, signal):
        step, sem, _ = self.queues[engine].pop()
        assert sem is None
        return self.do(engine, step, signal)

    def mark(self, signal):
        return signal, self.counts[signal]

    def wait(self, engine, *marks):
        for mark in marks:
            if mark is None:
                continue
            name, count = mark
            if self.waited.get((engine, name), 0) >= count:
                continue
            self.waited[engine, name] = count
            sem = self.sems[name]
            self.queues[engine].append((lambda e, s=sem, c=count: e.wait_ge(s, c), None, 0))

    def play(self, engine, e):
        for step, sem, by in self.queues[engine]:
            ins = step(e)
            if sem is not None:
                ins.then_inc(sem, by)


def build(nc, t):
    with ExitStack() as ctx:
        prog = Program(nc, ctx)
        ps = ctx.enter_context(nc.psum_tensor("ps", [P, 8, BANK], F32))
        k = Kernel(nc, t, prog, ctx, ps)
        with ExitStack() as stack:
            k.attention(stack)
        with ExitStack() as stack:
            k.experts(stack)
        block = ctx.enter_context(nc.Block())

        @block.sync
        def _(e):
            prog.play("sync", e)

        @block.scalar
        def _(e):
            prog.play("scalar", e)

        @block.vector
        def _(e):
            prog.play("vector", e)

        @block.gpsimd
        def _(e):
            prog.play("gpsimd", e)

        @block.tensor
        def _(e):
            prog.play("tensor", e)


class Kernel:

    def __init__(self, nc, t, prog, ctx, ps):
        self.nc, self.t, self.prog, self.ps = nc, t, prog, ps
        self.last_read = [None] * 8
        dram = lambda name, shape: nc.dram_tensor(name, shape, F32, kind="Internal").ap()
        self.x2_dram = dram("x2_rows", [TOK, D])
        self.rows_in = dram("expert_rows_in", [NROW, D])
        self.rows_out = dram("expert_rows_out", [NBLK * P, D])
        self.kspec_dram = dram("key_special_rows", [NH * DH, S])
        self.qspec_dram = dram("query_special_rows", [DH, S])
        sb = lambda name, shape, dt=F32: ctx.enter_context(nc.sbuf_tensor(name, shape, dt))
        self.ident = sb("ident", [P, P])
        self.steps = sb("steps", [P, P])
        self.zero_rows = sb("zero_rows", [P, D])
        self.slot = [sb(f"slot{k}", [P, NTT], I32) for k in range(TOPK)]
        self.result_row = [sb(f"result_row{k}", [P, NTT], I32) for k in range(TOPK)]
        self.weight = [sb(f"weight{k}", [P, NTT]) for k in range(TOPK)]
        self.expert_of = sb("expert_of", [P, NBLK], I32)
        self.row_of = sb("row_of", [P, NBLK], I32)

    def dma(self, step, signal, engine="sync"):
        return self.prog.do(engine, step, signal, 16)

    def pe_into(self, banks, *marks):
        self.prog.wait("tensor", *[self.last_read[b] for b in banks], *marks)

    def read_by(self, banks, mark):
        for b in banks:
            self.last_read[b] = mark

    def attention(self, stack):
        nc, t, prog, ps, ident, dma, pe_into, read_by = (
            self.nc, self.t, self.prog, self.ps, self.ident, self.dma, self.pe_into, self.read_by)
        do, wait = prog.do, prog.wait
        sb = lambda name, shape, dt=F32: stack.enter_context(nc.sbuf_tensor(name, shape, dt))
        flat = lambda ap: ap.rearrange("p a n -> p (a n)")

        hi = [sb(f"{a}_high", [P, DC, S], F32R) for a in "qk"]
        lo = [sb(f"{a}_low", [P, DC, S], F32R) for a in "qk"]
        wqkv = sb("wqkv", [P, DC, 3 * D])
        vt = [None, None]
        vt[0] = sb("values0", [P, NT, NH * VW + CT - VW])
        qa, ka = [None] * NSET, [None] * NSET
        for i in (1, 2, 0):
            qa[i] = sb(f"stacked_q{i}", [P, HG // 2, S], F32R)
            ka[i] = sb(f"stacked_k{i}", [P, HG, S], F32R)
        prob = sb("prob", [P, NPROB, 2, BANK])
        vt[1] = sb("values1", [P, NT, NH * VW + CT - VW])
        xr = sb("xr", [P, NT, D])
        xn = sb("xn", [P, NT, D])
        xT = sb("xT", [P, DC, S])
        on = sb("on", [P, NT, D])
        av = sb("av", [P, BANK])
        sc = sb("sc", [P, NT, CTX])
        pT = sb("pT", [CTX, BANK])
        wo, xwo = sb("wo", [P, DC, D]), sb("xwo", [P, DC, D])
        bqk = sb("bqk", [P, 2, DC])
        bv_all, bo_all, xbo_all = (sb(n, [P, D]) for n in ("bv_all", "bo_all", "xbo_all"))
        wr, br_all = sb("wr", [P, DC, NE]), sb("br_all", [P, NE])
        slopes = sb("slopes", [P, NH, P], F16)
        ramps = sb("ramps", [P, 2, BANK], F16)
        ones_row = sb("ones_row", [1, P])
        minus_half = sb("minus_half", [P, NT])
        ctx_keys = sb("ctx_keys", [P, NB, DC, CTX])
        ctx_vals = sb("ctx_vals", [CTX, NB, D])
        ctx_bias = sb("ctx_bias", [1, NB, CTX])
        stats, mv = sb("stats", [P, NT, 6]), sb("mv", [P, NT, 2])
        vep, rstd, shift = sb("vep", [P, NT]), sb("rstd", [P, NT]), sb("shift", [P, NT])
        rden = sb("rden", [P, 4 * HG])
        rmax, nmax = sb("rmax", [P, HG * NT, NCH]), sb("nmax", [P, HG * NT])
        nrow = sb("nrow", [HG * NT, P], F32R)
        smax, ssum = sb("smax", [P, NT]), sb("ssum", [P, NT])
        earlier, every = sb("earlier", [P, P]), sb("every", [P, P])
        pick_order = sb("pick_order", [P, NE])
        region = sb("region", [P, NE])
        count = sb("count", [P, NE])
        logits, rest, tmp, place = (sb(n, [P, NT, NE]) for n in ("logits", "rest", "tmp", "place"))
        upto = sb("upto", [P, NT + 1, NE])
        chosen = [sb(f"chosen{k}", [P, NT, NE]) for k in range(TOPK)]
        top = [sb(f"top{k}", [P, NT]) for k in range(TOPK)]
        first, slotf, wt = (sb(n, [P, NT]) for n in ("first", "slotf", "wt"))

        def load(signal, *pairs):
            for dst, src in pairs:
                m = dma(lambda e, dst=dst, src=src: e.dma_start(dst, src), signal)
            return m

        x_rows = lambda b: t["x"][b].rearrange("(t p) d -> p t d", p=P)
        x0_in = load("x0_in", (xr[:, :, :], x_rows(0)))

        def fetch_x(b):
            wait("gpsimd", *st["xr_free"])
            st["x_in"] = dma(lambda e: e.dma_start(xr[:, :, :], x_rows(b)), "x_in", "gpsimd")

        proj_in = load("proj_in", (ident[:, :], t["c_ident"]),
                       (wqkv[:, :, :], t["wqkv"].rearrange("(c p) n -> p c n", p=P)),
                       (bqk[:, :, :], t["bqk"]), (bv_all[:, :], t["bv"].broadcast_to([P, D])))
        do("vector", lambda e: e.memset(minus_half[:, :], -0.5), "dve_setup")
        first_set = do("vector", lambda e: e.memset(ones_row[:, :], 1.0), "dve_setup")

        st = {"unit": 0, "side": 0, "xT_free": [], "xn_free": [], "xr_free": [], "v": {}, "split": {},
              "prob_free": [None] * NPROB, "main": {}, "spread": {}, "on": {}, "av_free": None,
              "q_ready": {}, "x_in": x0_in}
        split = set()
        spread_next = [0]

        def side_bank():
            st["side"] += 1
            return 4 + st["side"] % 2

        def layer_norm(*ready):
            wait("vector", *ready)
            for tt in range(NT):
                m = do("vector", lambda e, tt=tt: e.bn_stats(stats[:, tt, :], xr[:, tt, :]), "dve_norm")
                if tt % 2:
                    yield
            wait("vector", m)
            for tt in range(NT):
                m = do("vector", lambda e, tt=tt: e.bn_aggr(mv[:, tt, :], stats[:, tt, :]), "dve_norm")
            wait("vector", m)
            m = do("vector", lambda e: e.tensor_scalar(vep[:, :], mv[:, :, 1], EPS, None, ALU.add), "dve_norm")
            wait("gpsimd", m)
            m = do("gpsimd", lambda e: e.tensor_tensor(rstd[:, :], vep[:, :], minus_half[:, :], ALU.pow), "pool_norm")
            yield from pause(2)
            wait("vector", m)
            m = do("vector", lambda e: e.scalar_tensor_tensor(
                out=shift[:, :], in0=mv[:, :, 0], scalar=-1.0, in1=rstd[:, :], op0=ALU.mult, op1=ALU.mult), "dve_norm")
            wait("scalar", m, *ready, *st["xn_free"])
            for tt in range(NT):
                m = do("scalar", lambda e, tt=tt: e.activation(
                    xn[:, tt, :], xr[:, tt, :], ACT.Identity, bias=shift[:, tt:tt + 1], scale=rstd[:, tt:tt + 1]), "act_norm")
                st["xn"] = m
                yield

        def pause(steps):
            for _ in range(steps):
                yield

        def turn(src, *ready):
            wait("scalar", *st["xT_free"])
            for c in range(DC):
                for four in range(NT // 4):
                    bank = side_bank()
                    pe_into([bank], *ready)
                    for q in range(4):
                        m = do("tensor", lambda e, c=c, tt=4 * four + q, q=q, bank=bank: e.transpose(
                            ps[:, bank, q * P:(q + 1) * P], src[:, tt, c * P:(c + 1) * P], ident[:, :]), "pe_turn")
                    wait("scalar", m)
                    st["xT"] = m2 = do("scalar", lambda e, c=c, four=four, bank=bank: e.activation(
                        xT[:, c, four * BANK:(four + 1) * BANK], ps[:, bank, :], ACT.Copy), "act_turn")
                    read_by([bank], m2)
                    yield
            st["turned"] = m
            yield

        def prepare(b):
            wait("gpsimd", first_set)
            yield from layer_norm(st["x_in"])
            st["xr_free"] = [st["xn"]]
            if b:
                fetch_x(b - 1)
            wait("tensor", proj_in)
            yield from turn(xn, st["xn"])
            st["xn_free"] = [st["turned"]]
            wait("tensor", st["xT"])
            wait("scalar", proj_in)
            wait("vector", proj_in)
            wait("scalar", st["spread"].get(NG * b - 1))
            wait("vector", st["spread"].get(NG * b - 1))
            if b == 0:
                wait("vector", proj_in)
                do("vector", lambda e: e.tensor_scalar(wqkv[:, :, 0:D], wqkv[:, :, 0:D], DH ** -0.5, None, ALU.mult), "dve_setup")
                scaled = do("vector", lambda e: e.tensor_scalar(bqk[:, 0, :], bqk[:, 0, :], DH ** -0.5, None, ALU.mult), "dve_setup")
                wait("tensor", scaled)
                wait("scalar", scaled)
                wait("vector", scaled)
            for mo in range(DC):
                for a in range(2):
                    for ch in range(NCH):
                        bank = side_bank()
                        pe_into([bank])
                        for c in range(DC):
                            m = do("tensor", lambda e, a=a, mo=mo, ch=ch, c=c, bank=bank: e.matmul(
                                ps[:, bank, :], wqkv[:, c, a * D + mo * P:a * D + (mo + 1) * P],
                                xT[:, c, ch * BANK:(ch + 1) * BANK], start=(c == 0), stop=(c == DC - 1)), "pe_proj")
                        cols = slice(ch * BANK, (ch + 1) * BANK)
                        wait("scalar", m)
                        mh = do("scalar", lambda e, a=a, mo=mo, cols=cols, bank=bank: e.activation(
                            hi[a][:, mo, cols], ps[:, bank, :], ACT.Identity, bias=bqk[:, a, mo:mo + 1]), "act_high")
                        wait("vector", mh)
                        st["split"][b] = ml = do("vector", lambda e, a=a, mo=mo, cols=cols, bank=bank: e.scalar_tensor_tensor(
                            out=lo[a][:, mo, cols], in0=ps[:, bank, :], scalar=bqk[:, a, mo:mo + 1],
                            in1=hi[a][:, mo, cols].bitcast(F32), op0=ALU.add, op1=ALU.subtract), "dve_low")
                        read_by([bank], ml)
                        yield
            split.add(b)
            spread_when_ready()
            for two in range(NT // 2):
                bank = side_bank()
                pe_into([bank])
                for k in range(2):
                    for c in range(DC):
                        m = do("tensor", lambda e, tt=2 * two + k, k=k, c=c, bank=bank: e.matmul(
                            ps[:, bank, k * D:(k + 1) * D], xT[:, c, tt * P:(tt + 1) * P], wqkv[:, c, 2 * D:3 * D],
                            start=(c == 0), stop=(c == DC - 1)), "pe_proj")
                wait("vector", m, st["main"].get(NG * (b - 1) - 1), v_ones)
                for k in range(2):
                    st["v"][b] = mv_ = do("vector", lambda e, tt=2 * two + k, k=k, bank=bank: e.tensor_tensor(
                        vt[b % 2][:, tt, 0:NH * VW].rearrange("p (h d) -> p h d", h=NH)[:, :, 0:DH],
                        ps[:, bank, k * D:(k + 1) * D].rearrange("p (h d) -> p h d", h=NH),
                        bv_all[:, :].rearrange("p (h d) -> p h d", h=NH), ALU.add), "dve_v")
                read_by([bank], mv_)
                yield
            st["xT_free"] = [m]

        def zeros_and_ones():
            for i in range(2):
                do("vector", lambda e, i=i: e.memset(vt[i][:, :, :], 1.0), "dve_fill")
            m_v, m = prog.mark("dve_fill"), None
            for i in range(NSET):
                for half in range(2):
                    r = HROWS * half
                    wait("gpsimd", m)
                    m = do("gpsimd", lambda e, i=i, r=r, half=half: e.memset(
                        ka[i][r:r + HROWS, 1 - half:HG:2, :].bitcast(F32), 0.0), "pool_fill")
            wait("gpsimd", m)
            return m_v, m

        v_ones, k_zeros = zeros_and_ones()

        def special_rows():
            kin = load("special_in", (kraw[:, :, :], t["c_kspec"].rearrange("(a p) n -> p a n", p=P)),
                       (qraw[:, :], t["c_qspec"]), (ramp_in[:, :, :], t["c_ramps"].rearrange("a p n -> p a n")),
                       (slope_in[:, :], t["c_slopes"].broadcast_to([P, NH])))
            wait("vector", kin, proj_in)
            do("vector", lambda e: e.tensor_copy(kround[:, :, :], kraw[:, :, :]), "dve_setup")
            do("vector", lambda e: e.tensor_copy(qround[:, :], qraw[:, :]), "dve_setup")
            m = prog.mark("dve_setup")
            wait("sync", m)
            back = load("special_out",
                        (self.kspec_dram.rearrange("(a p) n -> p a n", p=P), kround[:, :, :].bitcast(F32)),
                        (self.qspec_dram, qround[:, :].bitcast(F32)))
            do("vector", lambda e: e.tensor_copy(ramps[:, :, :], ramp_in[:, :, :]), "dve_setup")
            for h in range(NH):
                m = do("vector", lambda e, h=h: e.tensor_scalar(slopes[:, h, :], ident[:, :], slope_in[:, h:h + 1], None, ALU.mult), "dve_setup")
            return back, m

        kraw = prob[:, 0:2, :, :].rearrange("p a b n -> p (a b n)").rearrange("p (a n) -> p a n", a=2)
        kround = qa[2][:, 0:2, :]
        qraw = on[0:DH, 0:4, :].rearrange("p a n -> p (a n)")
        qround = qa[1][0:DH, 0, :]
        ramp_in = on[:, 4:8, :].rearrange("p a n -> p (a n)").rearrange("p (a n) -> p a n", a=2)
        slope_in = sc[:, 0, 0:NH]
        specials, slopes_done = special_rows()

        def context_products():
            NC = NB * CTX
            w = {n: flat(xn[:, 2 * i:2 * i + 2, :]).rearrange("p (c n) -> p c n", c=DC)
                 for i, n in enumerate(("xwk", "xwv", "xwq"))}
            cx = xr[:, 0:NB, :]
            cT, kT, vT = (flat(xT[:, :, :])[:, n * DC * NC:(n + 1) * DC * NC].rearrange("p (c n) -> p c n", c=DC)
                          for n in range(3))
            bias = {n: sc[:, 1, 2 * i:2 * i + 2] for i, n in enumerate(("xbq", "xbk", "xbv"))}
            wait("sync", slopes_done, specials, *st["xn_free"], *st["xr_free"], *st["xT_free"])
            wait("vector", *st["xT_free"])
            m_in = load("context_in", *[(w[n], t[n].rearrange("(c p) n -> p c n", p=P)) for n in w],
                        *[(bias[n], t[n]) for n in bias],
                        (cx[0:CTX, :, :], t["ctx"].rearrange("b c d -> c b d")),
                        (xwo[:, :, :], t["xwo"].rearrange("(c p) n -> p c n", p=P)))
            wait("tensor", m_in)
            for c in range(DC):
                bank = side_bank()
                pe_into([bank])
                for b in range(NB):
                    m = do("tensor", lambda e, b=b, c=c, bank=bank: e.transpose(
                        ps[:, bank, b * CTX:(b + 1) * CTX], cx[0:CTX, b, c * P:(c + 1) * P], ident[0:CTX, 0:CTX]), "pe_setup")
                wait("vector", m)
                m = do("vector", lambda e, c=c, bank=bank: e.tensor_copy(cT[:, c, :], ps[:, bank, 0:NC]), "dve_setup")
                read_by([bank], m)
                yield
            wait("tensor", m)
            for name, bname, out_ in (("xwk", "xbk", kT), ("xwv", "xbv", vT)):
                for mo in range(DC):
                    bank = side_bank()
                    pe_into([bank])
                    for c in range(DC):
                        m = do("tensor", lambda e, name=name, mo=mo, c=c, bank=bank: e.matmul(
                            ps[:, bank, 0:NC], w[name][:, c, mo * P:(mo + 1) * P], cT[:, c, :],
                            start=(c == 0), stop=(c == DC - 1)), "pe_setup")
                    wait("vector", m, m_in)
                    m = do("vector", lambda e, out_=out_, mo=mo, bank=bank, bname=bname: e.tensor_scalar(
                        out_[:, mo, :], ps[:, bank, 0:NC], bias[bname][:, mo:mo + 1], None, ALU.add), "dve_setup")
                    read_by([bank], m)
                    yield
            wait("tensor", m)
            for mo in range(DC):
                bank = side_bank()
                pe_into([bank])
                for c in range(DC):
                    m = do("tensor", lambda e, mo=mo, c=c, bank=bank: e.matmul(
                        ps[:, bank, 0:NC], w["xwq"][:, c, mo * P:(mo + 1) * P], kT[:, c, :],
                        start=(c == 0), stop=(c == DC - 1)), "pe_setup")
                wait("vector", m)
                m = do("vector", lambda e, mo=mo, bank=bank: e.tensor_copy(
                    ctx_keys[:, :, mo, :], ps[:, bank, 0:NC].rearrange("p (b j) -> p b j", b=NB)), "dve_setup")
                read_by([bank], m)
                yield
            bank = side_bank()
            pe_into([bank])
            for c in range(DC):
                m = do("tensor", lambda e, c=c, bank=bank: e.matmul(
                    ps[0:1, bank, 0:NC], bias["xbq"][:, c:c + 1], kT[:, c, :], start=(c == 0), stop=(c == DC - 1)), "pe_setup")
            wait("vector", m)
            m = do("vector", lambda e, bank=bank: e.tensor_copy(ctx_bias[:, :, :].rearrange("p b j -> p (b j)"), ps[0:1, bank, 0:NC]), "dve_setup")
            read_by([bank], m)
            for b in range(NB):
                bank = side_bank()
                pe_into([bank])
                for c in range(DC):
                    m = do("tensor", lambda e, b=b, c=c, bank=bank: e.matmul(
                        ps[0:CTX, bank, 0:D], vT[:, c, b * CTX:(b + 1) * CTX], xwo[:, c, :], start=(c == 0), stop=(c == DC - 1)), "pe_setup")
                st["xn_free"] = st["xr_free"] = [m]
                wait("vector", m)
                m = do("vector", lambda e, b=b, bank=bank: e.tensor_copy(ctx_vals[:, b, :], ps[0:CTX, bank, 0:D]), "dve_setup")
                read_by([bank], m)
                yield
            st["ctx_done"] = m
            fetch_x(1)
            st["xT_free"] = st["xn_free"]

        def spread(G):
            b, g, i = G // NG, G % NG, G % NSET
            wait("sync", st["split"][b], st["main"].get(G - NSET), k_zeros, specials, slopes_done)
            for hh in range(HG):
                h = g * HG + hh
                mo, r = h // 8, (h % 8) * DH
                base = HROWS * (hh % 2)
                q_rows = (self.qspec_dram, hi[0][r:r + DH, mo, :].bitcast(F32), lo[0][r:r + DH, mo, :].bitcast(F32),
                          hi[0][r:r + DH, mo, :].bitcast(F32))
                k_rows = (self.kspec_dram[h * DH:(h + 1) * DH, :], hi[1][r:r + DH, mo, :].bitcast(F32),
                          hi[1][r:r + DH, mo, :].bitcast(F32), lo[1][r:r + DH, mo, :].bitcast(F32))
                for j in range(4):
                    part = slice(base + DH * j, base + DH * (j + 1))
                    load(f"spread{i}", (qa[i][part, hh // 2, :].bitcast(F32), q_rows[j]))
                    m = load(f"spread{i}", (ka[i][part, hh, :].bitcast(F32), k_rows[j]))
            st["spread"][G] = m

        def spread_when_ready():
            while spread_next[0] < NB * NG:
                G = spread_next[0]
                if G >= NSET and G - NSET not in st["main"] or G // NG not in split:
                    return
                spread(G)
                spread_next[0] += 1

        def row_maxima(G):
            g, i = G % NG, G % NSET
            wait("tensor", st["spread"][G])
            for hh in range(HG):
                h = g * HG + hh
                for qt in range(NT):
                    for kc in range(NCH):
                        bank = side_bank()
                        pe_into([bank])
                        m = do("tensor", lambda e, hh=hh, qt=qt, kc=kc, bank=bank: e.matmul(
                            ps[:, bank, :], qa[i][:, hh // 2, qt * P:(qt + 1) * P],
                            ka[i][:, hh, kc * BANK:(kc + 1) * BANK], start=True, stop=True), "pe_max")
                        if qt // 4 == kc:
                            lo_, n, which, at = ((0, 256, 1, 0), (128, 128, 1, 0), (256, 128, 0, 384), (256, 256, 0, 256))[qt % 4]
                            m = do("tensor", lambda e, h=h, bank=bank, lo_=lo_, n=n, which=which, at=at: e.matmul(
                                ps[:, bank, lo_:lo_ + n], slopes[:, h, :], ramps[:, which, at:at + n],
                                start=False, stop=True, skip_group_check=True), "pe_max")
                        wait("vector", m)
                        m = do("vector", lambda e, n=hh * NT + qt, kc=kc, bank=bank: e.tensor_reduce(
                            rmax[:, n, kc:kc + 1], ps[:, bank, :], AX.X, ALU.max), "dve_max")
                        read_by([bank], m)
                        yield
            wait("vector", m)
            m = do("vector", lambda e: e.tensor_reduce(nmax[:, :], rmax[:, :, :], AX.X, ALU.max), "dve_max")
            bank = side_bank()
            pe_into([bank], m)
            m = do("tensor", lambda e, bank=bank: e.transpose(ps[0:HG * NT, bank, 0:P], nmax[:, :], ident[:, :]), "pe_max")
            wait("vector", m, st.get("nrow_free"))
            m = do("vector", lambda e, bank=bank: e.tensor_scalar(nrow[:, :], ps[0:HG * NT, bank, 0:P], -1.0, None, ALU.mult), "dve_max")
            read_by([bank], m)
            wait("sync", m)
            for hh in range(HG):
                row = HROWS * (hh % 2) + 2
                m = load("max_rows", (qa[i][row:row + 1, hh // 2, :].bitcast(F32), nrow[hh * NT:(hh + 1) * NT, :].bitcast(F32)))
            st["nrow_free"] = st["q_ready"][G] = m
            yield

        def main_pass(G, between):
            b, g, i = G // NG, G % NG, G % NSET
            wait("tensor", st["q_ready"][G], st["v"][b], slopes_done)

            def scores(ch, kt, two):
                u = st["unit"]
                st["unit"] += 1
                pair, slot = (u % 2) * 2, u % NPROB
                pe_into([pair, pair + 1])
                for k in range(2):
                    hh = two * 2 + k
                    m = do("tensor", lambda e, hh=hh, k=k: e.matmul(
                        ps[:, pair + k, :], ka[i][:, hh, kt * P:(kt + 1) * P],
                        qa[i][:, hh // 2, ch * BANK:(ch + 1) * BANK], start=True, stop=True), "pe_scores")
                    if kt // 4 == ch:
                        lo_, n, which, at = ((0, 128, 0, 384), (0, 256, 0, 256), (256, 256, 1, 0), (384, 128, 1, 0))[kt % 4]
                        m = do("tensor", lambda e, h=g * HG + hh, k=k: e.matmul(
                            ps[:, pair + k, lo_:lo_ + n], slopes[:, h, :], ramps[:, which, at:at + n],
                            start=False, stop=True, skip_group_check=True), "pe_scores")
                    if k == 0:
                        between(3 + two)
                wait("scalar", m, st["prob_free"][slot])
                m = do("scalar", lambda e: e.activation(prob[:, slot, :, :], ps[:, pair:pair + 2, :], ACT.Exp), "act_prob")
                read_by([pair, pair + 1], m)
                return slot, m

            def attend(ch, kt, made):
                bank = 6 + ch
                if kt == 0:
                    pe_into([bank])
                for two, (slot, ready) in enumerate(made):
                    wait("tensor", ready)
                    for k in range(2):
                        hh = two * 2 + k
                        c0 = (g * HG + hh) * VW
                        m = do("tensor", lambda e, hh=hh, k=k, c0=c0, slot=slot: e.matmul(
                            ps[CT * hh:CT * (hh + 1), bank, :], vt[b % 2][:, kt, c0:c0 + CT], prob[:, slot, k, :],
                            start=(kt == 0), stop=(kt == NT - 1)), "pe_attend")
                    st["prob_free"][slot] = m
                return m

            def finish(ch, m):
                bank = 6 + ch
                wait("scalar", m, st["av_free"])
                m = do("scalar", lambda e: e.activation(av[:, :], ps[:, bank, :], ACT.Copy), "act_av")
                read_by([bank], m)
                yield
                pe_into([bank], m)
                for q in range(4):
                    m = do("tensor", lambda e, q=q: e.transpose(
                        ps[:, bank, q * P:(q + 1) * P], av[:, q * P:(q + 1) * P], ident[:, :]), "pe_av")
                st["av_free"] = m
                yield
                wait("vector", m, *(st.get("on_free", []) if g == 0 else []))
                heads = ps[:, bank, :].rearrange("p (n c) -> p n c", c=CT)
                m = do("vector", lambda e: e.reciprocal(rden[:, :], heads[:, :, DH]), "dve_on")
                wait("vector", m)
                m = do("vector", lambda e: e.tensor_tensor(
                    on[:, 4 * ch:4 * ch + 4, g * HG * DH:(g + 1) * HG * DH].rearrange("p t (h d) -> p t h d", h=HG),
                    heads[:, :, 0:DH].rearrange("p (t h) d -> p t h d", h=HG),
                    rden[:, :].rearrange("p (t h) -> p t h", h=HG).unsqueeze(3).broadcast_to([P, 4, HG, DH]), ALU.mult), "dve_on")
                read_by([bank], m)
                wait("vector", m)
                st["on"][b] = m

            waiting, closing = [], []

            def close_one():
                if closing and next(closing[0], "end") == "end":
                    closing.pop(0)

            for ch in range(NCH):
                for kt in range(NT):
                    made = [scores(ch, kt, 0)]
                    between(0)
                    if waiting:
                        c_, k_, made_ = waiting.pop(0)
                        m = attend(c_, k_, made_)
                        if k_ == NT - 1:
                            closing.append(finish(c_, m))
                            close_one()
                    between(1)
                    made.append(scores(ch, kt, 1))
                    waiting.append((ch, kt, made))
                    between(2)
                    close_one()
            c_, k_, made_ = waiting.pop(0)
            st["main"][G] = m = attend(c_, k_, made_)
            closing.append(finish(c_, m))
            return closing

        def complete(b):
            if b == NB - 1:
                fetch_x(b)
            wait("gpsimd", st["x_in"], late_in)
            for tt in range(NT):
                xo = do("gpsimd", lambda e, tt=tt: e.tensor_tensor(xr[:, tt, :], xr[:, tt, :], bo_all[:, :], ALU.add), "pool_bias")
            yield from pause(4)
            yield from turn(on, st["on"][b])
            st["on_free"] = [st["turned"]]
            wait("tensor", st["xT"], late_in)
            wait("vector", xo)

            def add_rows(two, m, bank):
                wait("vector", m)
                m = do("vector", lambda e: e.tensor_tensor(
                    flat(xr[:, 2 * two:2 * two + 2, :]), ps[:, bank, :], flat(xr[:, 2 * two:2 * two + 2, :]), ALU.add), "dve_rows")
                read_by([bank], m)
                return m

            for two in range(NT // 2):
                bank = side_bank()
                pe_into([bank])
                for k in range(2):
                    for c in range(DC):
                        m = do("tensor", lambda e, tt=2 * two + k, k=k, c=c, bank=bank: e.matmul(
                            ps[:, bank, k * D:(k + 1) * D], xT[:, c, tt * P:(tt + 1) * P], wo[:, c, :],
                            start=(c == 0), stop=(c == DC - 1)), "pe_out")
                x1 = add_rows(two, m, bank)
                yield
            st["xT_free"] = [m]
            yield from layer_norm(x1)
            wait("gpsimd", st["xn"])
            for tt in range(NT):
                xo = do("gpsimd", lambda e, tt=tt: e.tensor_tensor(xr[:, tt, :], xr[:, tt, :], xbo_all[:, :], ALU.add), "pool_bias")
            yield from turn(xn, st["xn"])
            st["xn_free"] = [st["turned"]]
            wait("tensor", st["xT"], st["ctx_done"])
            for four in range(2):
                bank = side_bank()
                pe_into([bank])
                for q in range(4):
                    cols = slice(q * CTX, (q + 1) * CTX)
                    for c in range(DC):
                        do("tensor", lambda e, tt=4 * four + q, c=c, bank=bank, cols=cols: e.matmul(
                            ps[:, bank, cols], xT[:, c, tt * P:(tt + 1) * P], ctx_keys[:, b, c, :], start=(c == 0), stop=False))
                    m = do("tensor", lambda e, bank=bank, cols=cols: e.matmul(
                        ps[:, bank, cols], ones_row[:, :], ctx_bias[:, b, :], start=False, stop=True), "pe_ctx")
                wait("vector", m, st.get("sc_free"))
                part = slice(4 * four, 4 * four + 4)
                scv = ps[:, bank, 0:4 * CTX].rearrange("p (t j) -> p t j", t=4)
                m = do("vector", lambda e, part=part, scv=scv: e.tensor_reduce(smax[:, part], scv, AX.X, ALU.max), "dve_ctx")
                wait("vector", m)
                m = do("vector", lambda e, part=part, scv=scv: e.tensor_tensor(
                    sc[:, part, :], scv, smax[:, part].unsqueeze(2).broadcast_to([P, 4, CTX]), ALU.subtract), "dve_ctx")
                read_by([bank], m)
                yield
            wait("scalar", m)
            m = do("scalar", lambda e: e.activation(sc[:, :, :], sc[:, :, :], ACT.Exp, scale=D ** -0.5), "act_ctx")
            yield from pause(2)
            wait("vector", m)
            m = do("vector", lambda e: e.tensor_reduce(ssum[:, :], sc[:, :, :], AX.X, ALU.add), "dve_ctx")
            wait("vector", m)
            m = do("vector", lambda e: e.reciprocal(smax[:, :], ssum[:, :]), "dve_ctx")
            wait("vector", m)
            m = do("vector", lambda e: e.tensor_tensor(sc[:, :, :], sc[:, :, :], smax[:, :].unsqueeze(2).broadcast_to([P, NT, CTX]), ALU.mult), "dve_ctx")
            yield from pause(2)
            wait("vector", xo)
            sc_ready = m
            for two in range(NT // 2):
                if two % 2 == 0:
                    bank = side_bank()
                    pe_into([bank], sc_ready)
                    for q in range(4):
                        m = do("tensor", lambda e, tt=2 * two + q, q=q, bank=bank: e.transpose(
                            ps[0:CTX, bank, q * P:(q + 1) * P], sc[:, tt, :], ident[:, :]), "pe_ctx")
                    st["sc_free"] = m
                    wait("scalar", m, st.get("pT_free"))
                    mp = do("scalar", lambda e, bank=bank: e.activation(pT[:, :], ps[0:CTX, bank, :], ACT.Copy), "act_ctx")
                    read_by([bank], mp)
                    yield from pause(2)
                    wait("tensor", mp)
                bank = side_bank()
                pe_into([bank])
                for k in range(2):
                    for c in range(DC):
                        do("tensor", lambda e, tt=2 * two + k, k=k, c=c, bank=bank: e.matmul(
                            ps[:, bank, k * D:(k + 1) * D], xT[:, c, tt * P:(tt + 1) * P], xwo[:, c, :], start=(c == 0), stop=False))
                    m = do("tensor", lambda e, at=(2 * two + k) % 4, k=k, bank=bank: e.matmul(
                        ps[:, bank, k * D:(k + 1) * D], pT[:, at * P:(at + 1) * P], ctx_vals[:, b, :], start=False, stop=True), "pe_out")
                st["pT_free"] = m
                x2 = add_rows(two, m, bank)
                yield
            st["xT_free"] = [m]
            wait("sync", x2)
            stored = load("x2_out", (self.x2_dram[b * S:(b + 1) * S, :].rearrange("(t p) d -> p t d", p=P), xr[:, :, :]))
            yield from layer_norm(x2)
            st["xr_free"] = [st["xn"], stored]
            if b + 2 < NB:
                fetch_x(b + 2)
            yield from turn(xn, st["xn"])
            wait("tensor", st["xT"])
            bank = side_bank()
            pe_into([bank])
            for tt in range(NT):
                for c in range(DC):
                    m = do("tensor", lambda e, tt=tt, c=c, bank=bank: e.matmul(
                        ps[:, bank, tt * NE:(tt + 1) * NE], xT[:, c, tt * P:(tt + 1) * P], wr[:, c, :],
                        start=(c == 0), stop=(c == DC - 1)), "pe_out")
            st["xT_free"] = [m]
            yield from route(b, bank, m)

        def route(b, bank, logits_made):
            wait("vector", logits_made, late_in, route_in)

            def v(step):
                m = do("vector", step, "dve_route")
                wait("vector", m)
                return m

            bc = lambda a: a.unsqueeze(2).broadcast_to([P, NT, NE])
            be = lambda a: a.unsqueeze(1).broadcast_to([P, NT, NE])
            three = lambda a: a.rearrange("p (t n) -> p t n", n=NE)
            m = v(lambda e, bank=bank: e.tensor_tensor(logits[:, :, :], three(ps[:, bank, 0:NT * NE]), be(br_all[:, :]), ALU.add))
            read_by([bank], m)
            src = logits
            for k in range(TOPK):
                v(lambda e, k=k, src=src: e.tensor_reduce(top[k][:, :], src[:, :, :], AX.X, ALU.max))
                v(lambda e, k=k, src=src: e.tensor_tensor(tmp[:, :, :], src[:, :, :], bc(top[k][:, :]), ALU.is_equal))
                v(lambda e: e.tensor_tensor(tmp[:, :, :], tmp[:, :, :], be(pick_order[:, :]), ALU.mult))
                v(lambda e: e.tensor_reduce(first[:, :], tmp[:, :, :], AX.X, ALU.max))
                v(lambda e, k=k: e.tensor_tensor(chosen[k][:, :, :], bc(first[:, :]), be(pick_order[:, :]), ALU.is_equal))
                if k == 0:
                    v(lambda e: e.scalar_tensor_tensor(out=flat(rest[:, :, :]), in0=flat(chosen[0][:, :, :]), scalar=-3.0e38,
                                                       in1=flat(logits[:, :, :]), op0=ALU.mult, op1=ALU.add))
                    yield
                src = rest
            m = v(lambda e: e.tensor_tensor(tmp[:, :, :], chosen[0][:, :, :], chosen[1][:, :, :], ALU.add))
            bank = side_bank()
            pe_into([bank], m)
            do("tensor", lambda e, bank=bank: e.matmul(ps[:, bank, 0:NT * NE], earlier[:, :], flat(tmp[:, :, :]), start=True, stop=True))
            m = do("tensor", lambda e, bank=bank: e.matmul(ps[:, bank, NT * NE:2 * NT * NE], every[:, :], flat(tmp[:, :, :]), start=True, stop=True), "pe_route")
            m2 = v(lambda e: e.tensor_tensor(wt[:, :], top[1][:, :], top[0][:, :], ALU.subtract))
            wait("scalar", m2)
            m2 = do("scalar", lambda e: e.activation(wt[:, :], wt[:, :], ACT.Exp), "act_route")
            wait("vector", m, m2)
            tiles = slice(b * NT, (b + 1) * NT)
            v(lambda e: e.tensor_copy(upto[:, 0, :], count[:, :]))
            for tt in range(NT):
                v(lambda e, tt=tt, bank=bank: e.tensor_tensor(
                    upto[:, tt + 1, :], ps[:, bank, (NT + tt) * NE:(NT + tt + 1) * NE], upto[:, tt, :], ALU.add))
            m = v(lambda e, bank=bank: e.tensor_tensor(place[:, :, :], three(ps[:, bank, 0:NT * NE]), upto[:, 0:NT, :], ALU.add))
            read_by([bank], m)
            v(lambda e: e.tensor_copy(count[:, :], upto[:, NT, :]))
            v(lambda e: e.tensor_tensor(place[:, :, :], place[:, :, :], be(region[:, :]), ALU.add))
            for k in range(TOPK):
                v(lambda e, k=k: e.tensor_tensor(tmp[:, :, :], place[:, :, :], chosen[k][:, :, :], ALU.mult))
                v(lambda e: e.tensor_reduce(slotf[:, :], tmp[:, :, :], AX.X, ALU.add))
                slots = v(lambda e, k=k: e.tensor_copy(self.slot[k][:, tiles], slotf[:, :]))
            v(lambda e: e.tensor_scalar(first[:, :], wt[:, :], 1.0, None, ALU.add))
            v(lambda e: e.reciprocal(self.weight[0][:, tiles], first[:, :]))
            st["routed"] = v(lambda e: e.tensor_tensor(self.weight[1][:, tiles], self.weight[0][:, tiles], wt[:, :], ALU.mult))
            yield
            wait("gpsimd", slots)
            for tt in range(NT):
                for k in range(TOPK):
                    self.scattered = dma(lambda e, tt=tt, k=k: e.indirect_dma_start(
                        self.rows_in, bass.IndirectOffsetOnAxis(ap=self.slot[k][:, b * NT + tt:b * NT + tt + 1], axis=0),
                        xn[:, tt, :], None), "scattered", "gpsimd")
                if tt % 4 == 3:
                    yield
            st["xn_free"] = [st["turned"], self.scattered]

        for _ in prepare(0):
            pass
        late_in = load("late_in", (wo[:, :, :], t["wo"].rearrange("(c p) n -> p c n", p=P)),
                       (bo_all[:, :], t["bo"].broadcast_to([P, D])), (xbo_all[:, :], t["xbo"].broadcast_to([P, D])),
                       (wr[:, :, :], t["wr"].rearrange("(c p) n -> p c n", p=P)), (br_all[:, :], t["br"].broadcast_to([P, NE])),
                       (earlier[:, :], t["c_low"]), (self.steps[:, :], t["c_first"]))
        maxima = row_maxima(0)
        products = context_products()
        wait("vector", slopes_done)
        wait("tensor", slopes_done)
        busy = True
        while busy:
            busy = False
            for _ in range(4):
                busy |= next(maxima, "end") != "end"
            busy |= next(products, "end") != "end"
        wait("vector", late_in)
        do("vector", lambda e: e.memset(every[:, :], 1.0), "dve_setup")
        do("vector", lambda e: e.memset(count[:, :], 0.0), "dve_setup")
        zeroed = do("vector", lambda e: e.memset(self.zero_rows[:, :], 0.0), "dve_setup")
        do("vector", lambda e: e.tensor_scalar(pick_order[:, :], self.steps[:, 0:NE], -1.0 / P, float(NE), ALU.mult, ALU.add), "dve_setup")
        route_in = do("vector", lambda e: e.tensor_scalar(region[:, :], self.steps[:, 0:NE], float(REGION // P), None, ALU.mult), "dve_setup")
        wait("sync", zeroed)
        for n in range(NIDLE):
            self.idle_zeroed = load("idle_zeroed", (self.rows_in[NE * REGION + n * P:NE * REGION + (n + 1) * P, :], self.zero_rows[:, :]))

        def background():
            for b in range(NB):
                if b:
                    yield from complete(b - 1)
                while len(st["main"]) < NG * b + 1:
                    yield "idle"
                if b + 1 < NB:
                    yield from prepare(b + 1)
                while len(st["main"]) < NG * (b + 1):
                    yield "idle"

        back = background()
        closing = []
        for G in range(NB * NG):
            maxima = row_maxima(G + 1) if G + 1 < NB * NG else iter(())

            def between(where):
                nonlocal closing
                for _ in range(MAXIMA[where]):
                    next(maxima, None)
                if closing and next(closing[0], "end") == "end":
                    closing.pop(0)
                if where < 3:
                    next(back, None)

            closing = main_pass(G, between)
            for _ in maxima:
                pass
            spread_when_ready()
            if G < NB * NG - 1:
                self.prefetch(G, st)
        for c in closing:
            for _ in c:
                pass
        for _ in back:
            pass
        last = complete(NB - 1)
        next(last)
        self.prefetch(NB * NG - 1, st)
        for _ in last:
            pass

        idle = on[:, :, :].rearrange("p t d -> p (t d)")
        past = idle[:, 0:NBLK * NE].rearrange("p (b n) -> p b n", n=NE)
        past_blocks = idle[:, NBLK * NE:2 * NBLK * NE].rearrange("p (b n) -> p b n", n=NE)
        blocks_gt = idle[:, 2 * NBLK * NE:2 * NBLK * NE + NE * NTT].rearrange("p (n b) -> p n b", n=NE)
        nblocks, end, zrow = sb("nblocks", [P, NE]), sb("end", [P, NE + 1]), sb("zrow", [P, NE], I32)
        used = 2 * NBLK * NE + NE * NTT
        at_in, at_out, moved = (idle[:, used + i * NTT:used + (i + 1) * NTT] for i in range(3))
        used += 3 * NTT
        ended, row = (idle[:, used + i * NBLK:used + (i + 1) * NBLK] for i in range(2))

        def v(step):
            m = do("vector", step, "dve_route")
            wait("vector", m)
            return m

        v(lambda e: e.tensor_scalar(end[:, 0:NE], count[:, :], self.steps[:, P - 1:P], None, ALU.add))
        zero_at = v(lambda e: e.tensor_tensor(zrow[:, :], end[:, 0:NE], region[:, :], ALU.add))
        wait("gpsimd", zero_at)
        for n in range(NE):
            self.scattered = dma(lambda e, n=n: e.indirect_dma_start(
                self.rows_in, bass.IndirectOffsetOnAxis(ap=zrow[:, n:n + 1], axis=0), self.zero_rows[:, :], None), "scattered", "gpsimd")
        v(lambda e: e.tensor_tensor(blocks_gt[:, :, :], count[:, :].unsqueeze(2).broadcast_to([P, NE, NTT]),
                                    self.steps[:, 0:NTT].unsqueeze(1).broadcast_to([P, NE, NTT]), ALU.is_gt))
        v(lambda e: e.tensor_reduce(nblocks[:, :], blocks_gt[:, :, :], AX.X, ALU.add))
        v(lambda e: e.memset(end[:, 0:1], 0.0))
        for n in range(NE):
            v(lambda e, n=n: e.tensor_tensor(end[:, n + 1:n + 2], end[:, n:n + 1], nblocks[:, n:n + 1], ALU.add))
        v(lambda e: e.tensor_scalar(row[:, :], self.steps[:, 0:NBLK], 1.0 / P, None, ALU.mult))
        v(lambda e: e.tensor_tensor(past[:, :, :], row[:, :].unsqueeze(2).broadcast_to([P, NBLK, NE]),
                                    end[:, 1:NE + 1].unsqueeze(1).broadcast_to([P, NBLK, NE]), ALU.is_ge))
        v(lambda e: e.tensor_reduce(ended[:, :], past[:, :, :], AX.X, ALU.add))
        v(lambda e: e.tensor_tensor(past_blocks[:, :, :], past[:, :, :], nblocks[:, :].unsqueeze(1).broadcast_to([P, NBLK, NE]), ALU.mult))
        v(lambda e: e.tensor_reduce(row[:, :], past_blocks[:, :, :], AX.X, ALU.add))
        v(lambda e: e.tensor_scalar(row[:, :], row[:, :], -float(P), None, ALU.mult))
        v(lambda e: e.tensor_tensor(row[:, :], row[:, :], self.steps[:, 0:NBLK], ALU.add))
        v(lambda e: e.scalar_tensor_tensor(out=self.row_of[:, :], in0=ended[:, :], scalar=float(REGION), in1=row[:, :], op0=ALU.mult, op1=ALU.add))
        self.blocks_known = v(lambda e: e.tensor_scalar(self.expert_of[:, :], ended[:, :], float(NE - 1), None, ALU.min))
        v(lambda e: e.tensor_scalar(nblocks[:, :], nblocks[:, :], float(P), -float(REGION), ALU.mult, ALU.add))
        for k in range(TOPK):
            v(lambda e, k=k: e.tensor_copy(at_in[:, :], self.slot[k][:, :]))
            v(lambda e, k=k: e.tensor_copy(at_out[:, :], at_in[:, :]))
            for n in range(1, NE):
                v(lambda e, n=n: e.tensor_scalar(moved[:, :], at_in[:, :], float(n * REGION), nblocks[:, n - 1:n], ALU.is_ge, ALU.mult))
                v(lambda e: e.tensor_tensor(at_out[:, :], at_out[:, :], moved[:, :], ALU.add))
            self.results_known = v(lambda e, k=k: e.tensor_copy(self.result_row[k][:, :], at_out[:, :]))
        self.attention_end = [st["routed"], self.scattered, self.idle_zeroed, st["main"][NB * NG - 1],
                              st["xr_free"][1], st["x_in"], self.results_known, st["turned"]]

    def prefetch(self, G, st):
        last = NB * NG - 1
        parts = {last - 3: [("w1", n) for n in range(5)], last - 2: [("w1", n) for n in range(5, 8)],
                 last - 1: [("w2", n) for n in range(3)], last: [("w2", n) for n in range(3, 8)]}.get(G, [])
        if parts:
            self.prog.wait("sync", st["main"][G], st["spread"][last])
        for name, n in parts:
            self.weights_in = self.dma(lambda e, name=name, n=n: e.dma_start(
                self.w[name][:, n, :, :], self.t[name][n].rearrange("(c p) f -> p c f", p=P)), "experts_in")

    def experts(self, stack):
        nc, t, prog, ps, ident, dma, pe_into, read_by = (
            self.nc, self.t, self.prog, self.ps, self.ident, self.dma, self.pe_into, self.read_by)
        do, wait, slot, weight = prog.do, prog.wait, self.slot, self.weight
        alloc = lambda stack, name, shape, dt=F32: stack.enter_context(nc.sbuf_tensor(name, shape, dt))
        w1 = alloc(stack, "w1", [P, NE, DC, FF])
        w2 = alloc(stack, "w2", [P, NE, FC, D])
        self.w = {"w1": w1, "w2": w2}
        b1_all = alloc(stack, "b1_all", [P, NE, FF])
        b2_all = alloc(stack, "b2_all", [P, NE, D])
        wait("sync", *self.attention_end)
        for dst, name in ((b1_all, "b1"), (b2_all, "b2")):
            experts_in = dma(lambda e, dst=dst, name=name: e.dma_start(
                dst[:, :, :].rearrange("p n f -> p (n f)"), t[name].broadcast_to([P, dst.shape[1] * dst.shape[2]])), "experts_in")
        blocks_known = self.blocks_known

        NX = 3
        bk = ExitStack()
        sb = lambda name, shape, dt=F32: alloc(bk, name, shape, dt)
        xi = [sb(f"xi{i}", [P, D]) for i in range(NX)]
        xiT = [sb(f"xiT{i}", [P, DC, P]) for i in range(2)]
        hid = [sb(f"hid{i}", [P, FF]) for i in range(2)]
        hidT = [sb(f"hidT{i}", [P, FC, P]) for i in range(2)]
        yo = [sb(f"yo{i}", [P, D]) for i in range(2)]
        wait("tensor", blocks_known, experts_in)
        wait("vector", *self.attention_end, experts_in)
        wait("scalar", *self.attention_end)
        regs = {}
        rd = {}

        def load_block(n):
            wait("sync", rd.get(("xi", n - NX)))
            rd["in", n] = dma(lambda e, n=n: e.dma_start(
                xi[n % NX][:, :], self.rows_in[bass.ds(read_value(e, self.row_of, n, NROW - P), P), :]), f"slots_in{n % NX}")

        def turn_block(n):
            pe_into([0], rd["in", n])
            for c in range(DC):
                m = do("tensor", lambda e, n=n, c=c: e.transpose(ps[:, 0, c * P:(c + 1) * P], xi[n % NX][:, c * P:(c + 1) * P], ident[:, :]), "pe_x")
            rd["xi", n] = m
            wait("scalar", m, rd.get(("up", n - 2)))
            rd["xiT", n] = m = do("scalar", lambda e, n=n: e.activation(xiT[n % 2][:, :, :].rearrange("p c n -> p (c n)"), ps[:, 0, 0:D], ACT.Copy), "act_x")
            read_by([0], m)

        def up(n, half):
            bank = 1 + 2 * (n % 2) + half
            pe_into([bank], rd["xiT", n])
            if half == 0:
                do("tensor", lambda e, n=n: regs.__setitem__(("t", n), read_value(e, self.expert_of, n, NE - 1)))
            for c in range(DC):
                m = do("tensor", lambda e, n=n, c=c, bank=bank, half=half: e.matmul(
                    ps[:, bank, :], xiT[n % 2][:, c, :], w1[:, bass.ds(regs["t", n], 1), c, half * BANK:(half + 1) * BANK].rearrange("p a f -> p (a f)"),
                    start=(c == 0), stop=(c == DC - 1)), "pe_up")
            rd["up", n] = m
            if half == 0:
                do("vector", lambda e, n=n: regs.__setitem__(("v", n), read_value(e, self.expert_of, n, NE - 1)))
            wait("vector", m, rd.get(("turn", n - 2)))
            rd["hid", n] = m = do("vector", lambda e, n=n, half=half, bank=bank: e.tensor_tensor(
                hid[n % 2][:, half * BANK:(half + 1) * BANK], ps[:, bank, :],
                b1_all[:, bass.ds(regs["v", n], 1), half * BANK:(half + 1) * BANK].rearrange("p a f -> p (a f)"), ALU.add), "dve_up")
            read_by([bank], m)

        def turn_hidden(n):
            pe_into([5, 6], rd["hid", n])
            for c in range(FC):
                m = do("tensor", lambda e, n=n, c=c: e.transpose(ps[:, 5 + c // 4, (c % 4) * P:(c % 4 + 1) * P], hid[n % 2][:, c * P:(c + 1) * P], ident[:, :]), "pe_h")
            rd["turn", n] = m
            wait("scalar", m, rd.get(("down", n - 2)))
            rd["hidT", n] = m = do("scalar", lambda e, n=n: e.activation(
                hidT[n % 2][:, :, :].rearrange("p c n -> p (c n)"), ps[:, 5:7, :].rearrange("p a n -> p (a n)"), ACT.Relu), "act_h")
            read_by([5, 6], m)

        def down(n):
            pe_into([7], rd["hidT", n])
            for c in range(FC):
                m = do("tensor", lambda e, n=n, c=c: e.matmul(
                    ps[:, 7, 0:D], hidT[n % 2][:, c, :], w2[:, bass.ds(regs["t", n], 1), c, :].rearrange("p a f -> p (a f)"),
                    start=(c == 0), stop=(c == FC - 1)), "pe_down")
            rd["down", n] = m
            wait("vector", m, rd.get(("out", n - 2)))
            m = do("vector", lambda e, n=n: e.tensor_tensor(
                yo[n % 2][:, :], ps[:, 7, 0:D], b2_all[:, bass.ds(regs["v", n], 1), :].rearrange("p a f -> p (a f)"), ALU.add), "dve_down")
            read_by([7], m)
            wait("sync", m)
            rd["out", n] = dma(lambda e, n=n: e.dma_start(
                self.rows_out[n * P:(n + 1) * P, :], yo[n % 2][:, :]), f"slots_out{n % 2}")

        for n in range(min(NX, NBLK)):
            load_block(n)
        turn_block(0)
        up(0, 0)
        up(0, 1)
        turn_block(1)
        for n in range(NBLK):
            if n + 1 < NBLK:
                up(n + 1, 0)
            turn_hidden(n)
            if n + 1 < NBLK:
                up(n + 1, 1)
            if n + 2 < NBLK:
                turn_block(n + 2)
            if n + NX < NBLK:
                load_block(n + NX)
            down(n)

        bk.close()

        NO = 4
        sb = lambda name, shape, dt=F32: alloc(stack, name, shape, dt)
        got = [sb(f"got{i}", [P, TOPK, D]) for i in range(NO)]
        res = [sb(f"res{i}", [P, D]) for i in range(NO)]
        wait("gpsimd", rd["out", NBLK - 1], rd["out", NBLK - 2], self.results_known)
        wait("sync", rd["out", NBLK - 1], rd["out", NBLK - 2])
        for tt in range(NTT):
            i = tt % NO
            wait("gpsimd", rd.get(("sum", tt - NO)))
            for k in range(TOPK):
                mg = dma(lambda e, i=i, k=k, tt=tt: e.indirect_dma_start(
                    got[i][:, k, :], None, self.rows_out, bass.IndirectOffsetOnAxis(ap=self.result_row[k][:, tt:tt + 1], axis=0)), f"gathered{i}", "gpsimd")
            wait("sync", rd.get(("outd", tt - NO)))
            ml = dma(lambda e, i=i, tt=tt: e.dma_start(res[i][:, :], self.x2_dram[tt * P:(tt + 1) * P, :]), f"x2_back{i}")
            wait("vector", mg, ml)
            for k in range(TOPK):
                m = do("vector", lambda e, i=i, k=k, tt=tt: e.scalar_tensor_tensor(
                    out=res[i][:, :], in0=got[i][:, k, :], scalar=weight[k][:, tt:tt + 1], in1=res[i][:, :], op0=ALU.mult, op1=ALU.add), "dve_sum")
                if k == 0:
                    wait("vector", m)
            rd["sum", tt] = m
            wait("scalar", m)
            rd["outd", tt] = dma(lambda e, i=i, tt=tt: e.dma_start(t["out"][tt * P:(tt + 1) * P, :], res[i][:, :]), f"result{i}", "scalar")
        for i in range(NO):
            wait("scalar", rd["outd", NTT - NO + i])



def read_value(e, table, n, most):
    return e.value_load(table[0:1, n:n + 1], min_val=0, max_val=most)


def constants():
    slopes = 0.5 ** np.arange(NH)
    pos = np.arange(S)
    tile = pos // P
    kspec = np.zeros((NH, DH, S), np.float32)
    qspec = np.zeros((DH, S), np.float32)
    for c in range(NCH):
        sign = np.where(tile < 4 * c + 2, 1.0, -1.0)
        inside = (tile // 4 == c).astype(np.float32)
        kspec[:, 3 * c, :] = slopes[:, None] * (sign * pos)[None, :]
        kspec[:, 3 * c + 1, :] = -slopes[:, None] * sign[None, :]
        qspec[3 * c], qspec[3 * c + 1] = inside, pos * inside
    kspec[:, 2, :] = 1.0
    p, f = np.arange(P)[:, None], np.arange(BANK)[None, :]
    ramps = np.stack([-2.0 * np.maximum(0, p + BANK - P - f), -2.0 * np.maximum(0, f - p)]) / 16.0
    first = np.tile(np.arange(P, dtype=np.float32)[None, :] * P, (P, 1))
    first[:, P - 1] = np.arange(P)
    return {
        "c_ident": np.eye(P, dtype=np.float32),
        "c_kspec": kspec.reshape(NH * DH, S),
        "c_slopes": (16.0 * slopes).astype(np.float32)[None, :],
        "c_ramps": ramps.astype(np.float32),
        "c_qspec": qspec,
        "c_low": (np.arange(P)[:, None] < np.arange(P)[None, :]).astype(np.float32),
        "c_first": first,
    }


def kernel(**inputs):
    import concourse.bacc as bacc
    from concourse.bass_utils import run_bass_kernel_spmd

    a = {k: np.asarray(v) for k, v in inputs.items()}
    qkv = a["L0_attn_qkv_w"].reshape(NH, 3, DH, D).transpose(3, 1, 0, 2).reshape(D, 3 * D)
    qkv_b = a["L0_attn_qkv_b"].reshape(NH, 3, DH).transpose(1, 0, 2).reshape(3, D)
    row = lambda v: v.reshape(1, -1)
    col = lambda v: v.reshape(DC, P).T
    arrays = {
        "x": a["x"], "ctx": a["ctx_1024"],
        "wqkv": qkv, "bqk": qkv_b[0:2].reshape(2, DC, P).transpose(2, 0, 1), "bv": qkv_b[2:3],
        "wo": a["L0_attn_out_w"].T, "bo": row(a["L0_attn_out_b"]),
        "xwo": a["L0_xattn_Wo"].T, "xbo": row(a["L0_xattn_bo"]),
        "xwq": a["L0_xattn_Wq"], "xwk": a["L0_xattn_Wk"].T, "xwv": a["L0_xattn_Wv"].T,
        "xbq": col(a["L0_xattn_bq"]), "xbk": col(a["L0_xattn_bk"]), "xbv": col(a["L0_xattn_bv"]),
        "wr": a["L0_ffn_W_router"], "br": row(a["L0_ffn_b_router"]),
        "w1": a["L0_ffn_W1"], "b1": row(a["L0_ffn_b1"]), "w2": a["L0_ffn_W2"], "b2": row(a["L0_ffn_b2"]),
        **constants(),
    }
    arrays = {k: np.ascontiguousarray(v) for k, v in arrays.items()}
    nc = bacc.Bacc("TRN2", target_bir_lowering=False, num_devices=1)
    t = {k: nc.dram_tensor("in_" + k, v.shape, mybir.dt.from_np(v.dtype), kind="ExternalInput").ap()
         for k, v in arrays.items()}
    t["out"] = nc.dram_tensor("out", [TOK, D], F32, kind="ExternalOutput").ap()
    build(nc, t)
    r = run_bass_kernel_spmd(nc, [{"in_" + k: v for k, v in arrays.items()}], core_ids=[0])
    return r.results[0]["out"].reshape(NB, S, D)
```

```python
from contextlib import ExitStack
from itertools import chain

import numpy as np
import concourse.bass as bass
from concourse import mybir

F32 = mybir.dt.float32
F32R = mybir.dt.float32r
F16 = mybir.dt.float16
I32 = mybir.dt.int32
ALU = mybir.AluOpType
ACT = mybir.ActivationFunctionType
AX = mybir.AxisListType

P = 128
NB, S, D = 4, 1024, 256
NH, DH = 16, 16
CTX = 77
NE, FF = 8, 1024
TOPK = 2
EPS = 1e-5
NT = S // P
DC = D // P
FC = FF // P
BANK = 512
NCH = S // BANK
HG = 4
NG = NH // HG
HROWS = 64
TOK = NB * S
NTT = TOK // P
NBLK = (TOK * TOPK) // P + NE - 1
REGION = TOK + P
NIDLE = NE - 1
NROW = NE * REGION + NIDLE * P
VW = DH + 1
CT = 32
TOKEN, CODE, SECOND, MORE = range(D, D + 4)
SENT = D + 4
NSUB = S // (2 * P)
MAX_ROW = 2 * NSUB
NSET = 3
NSCORE, NSIDE = 3, 3
NPROB = 6
PLACES = 5 * NCH * NT
MAXIMA_END = PLACES - 8


class Program:

    def __init__(self, nc, ctx):
        self.nc, self.ctx = nc, ctx
        self.queues = {e: [] for e in ("tensor", "vector", "scalar", "gpsimd", "sync")}
        self.sems, self.counts, self.waited = {}, {}, {}

    def do(self, engine, step, signal=None, by=1):
        sem = None
        if signal is not None:
            if signal not in self.sems:
                self.sems[signal] = self.ctx.enter_context(self.nc.semaphore(signal))
                self.counts[signal] = 0
            sem = self.sems[signal]
            self.counts[signal] += by
        self.queues[engine].append((step, sem, by))
        return (signal, self.counts[signal]) if signal is not None else None

    def mark(self, signal):
        return signal, self.counts[signal]

    def wait(self, engine, *marks):
        for mark in marks:
            if mark is None:
                continue
            name, count = mark
            if self.waited.get((engine, name), 0) >= count:
                continue
            self.waited[engine, name] = count
            sem = self.sems[name]
            self.queues[engine].append((lambda e, s=sem, c=count: e.wait_ge(s, c), None, 0))

    def play(self, engine, e):
        for step, sem, by in self.queues[engine]:
            ins = step(e)
            if sem is not None:
                ins.then_inc(sem, by)


def build(nc, t):
    with ExitStack() as ctx:
        prog = Program(nc, ctx)
        ps = ctx.enter_context(nc.psum_tensor("ps", [P, 8, BANK], F32))
        k = Kernel(nc, t, prog, ctx, ps)
        with ExitStack() as stack:
            k.attention(stack)
        with ExitStack() as stack:
            k.experts(stack)
        block = ctx.enter_context(nc.Block())

        @block.sync
        def _(e):
            prog.play("sync", e)

        @block.scalar
        def _(e):
            prog.play("scalar", e)

        @block.vector
        def _(e):
            prog.play("vector", e)

        @block.gpsimd
        def _(e):
            prog.play("gpsimd", e)

        @block.tensor
        def _(e):
            prog.play("tensor", e)


class Kernel:

    def __init__(self, nc, t, prog, ctx, ps):
        self.nc, self.t, self.prog, self.ps = nc, t, prog, ps
        self.last_read = [None] * 8
        dram = lambda name, shape: nc.dram_tensor(name, shape, F32, kind="Internal").ap()
        self.rows_in = dram("expert_rows", [NROW, SENT])
        self.kspec_dram = dram("key_special_rows", [NH * DH, S])
        self.qspec_dram = dram("query_special_rows", [DH, S])
        sb = lambda name, shape, dt=F32: ctx.enter_context(nc.sbuf_tensor(name, shape, dt))
        self.ident = sb("ident", [P, P])
        self.steps = sb("steps", [P, P])
        self.no_rows = sb("no_rows", [P, SENT])
        self.slot = [sb(f"slot{k}", [P, NTT], I32) for k in range(TOPK)]
        self.expert_of = sb("expert_of", [P, NBLK], I32)
        self.code_of = sb("code_of", [P, NBLK])
        self.row_of = sb("row_of", [P, NBLK], I32)

    def dma(self, step, signal, engine="sync"):
        return self.prog.do(engine, step, signal, 16)

    def pe_into(self, banks, *marks):
        self.prog.wait("tensor", *[self.last_read[b] for b in banks], *marks)

    def read_by(self, banks, mark):
        for b in banks:
            self.last_read[b] = mark

    def attention(self, stack):
        nc, t, prog, ps, ident, dma, pe_into, read_by = (
            self.nc, self.t, self.prog, self.ps, self.ident, self.dma, self.pe_into, self.read_by)
        do, wait = prog.do, prog.wait
        sb = lambda name, shape, dt=F32: stack.enter_context(nc.sbuf_tensor(name, shape, dt))
        flat = lambda ap: ap.rearrange("p a n -> p (a n)")

        hi = [sb(f"{a}_high", [P, DC, S], F32R) for a in "qk"]
        lo = [sb(f"{a}_low", [P, DC, S], F32R) for a in "qk"]
        wqkv = sb("wqkv", [P, DC, 3 * D])
        vt = [None, None]
        vt[0] = sb("values0", [P, NT, NH * VW + CT - VW])
        qa, ka = [None] * NSET, [None] * NSET
        for i in (1, 2, 0):
            qa[i] = sb(f"stacked_q{i}", [P, HG // 2, S], F32R)
            ka[i] = sb(f"stacked_k{i}", [P, HG, S], F32R)
        prob = sb("prob", [P, NPROB, BANK])
        vt[1] = sb("values1", [P, NT, NH * VW + CT - VW])
        xr = sb("xr", [P, NT, D])
        xn = sb("xn", [P, NT, SENT])
        xT = sb("xT", [P, DC, S])
        on = sb("on", [P, NT, D])
        av = sb("av", [P, BANK])
        sc = sb("sc", [P, NT, CTX])
        pT = sb("pT", [CTX, BANK])
        wo, xwo = sb("wo", [P, DC, D]), sb("xwo", [P, DC, D])
        bqk = sb("bqk", [P, 2, DC])
        bv_all, bo_all, xbo_all = (sb(n, [P, D]) for n in ("bv_all", "bo_all", "xbo_all"))
        wr, br_all = sb("wr", [P, DC, NE]), sb("br_all", [P, NE])
        slopes = sb("slopes", [P, NH, P], F16)
        ramps = sb("ramps", [P, 2, P], F16)
        ones_row = sb("ones_row", [1, P])
        minus_half = sb("minus_half", [P, NT])
        ctx_keys = sb("ctx_keys", [P, NB, DC, CTX])
        ctx_vals = sb("ctx_vals", [CTX, NB, D])
        ctx_bias = sb("ctx_bias", [1, NB, CTX])
        stats, mv = sb("stats", [P, NT, 6]), sb("mv", [P, NT, 2])
        varp, rstd, shift = sb("varp", [P, NT]), sb("rstd", [P, NT]), sb("shift", [P, NT])
        rden = sb("rden", [P, 4 * HG])
        rmax, nmax = sb("rmax", [P, HG * NT, NCH]), sb("nmax", [P, HG * NT])
        nrow = sb("nrow", [HG * NT, P], F32R)
        smax, ssum = sb("smax", [P, NT]), sb("ssum", [P, NT])
        earlier, every = sb("earlier", [P, P]), sb("every", [P, P])
        pick_order = sb("pick_order", [P, NE])
        region = sb("region", [P, NE])
        count = sb("count", [P, NE])
        logits, rest, tmp, place = (sb(n, [P, NT, NE]) for n in ("logits", "rest", "tmp", "place"))
        upto = sb("upto", [P, NT + 1, NE])
        chosen = [sb(f"chosen{k}", [P, NT, NE]) for k in range(TOPK)]
        top = [sb(f"top{k}", [P, NT]) for k in range(TOPK)]
        first, slotf, wt, code = (sb(n, [P, NT]) for n in ("first", "slotf", "wt", "code"))

        def load(signal, *pairs, engine="sync"):
            for dst, src in pairs:
                m = dma(lambda e, dst=dst, src=src: e.dma_start(dst, src), signal, engine)
            return m

        x_rows = lambda b: t["x"][b].rearrange("(t p) d -> p t d", p=P)
        x0_in = [load(f"x0_in{i}", (xr[:, 2 * i:2 * i + 2, :], x_rows(0)[:, 2 * i:2 * i + 2, :])) for i in range(NT // 2)]

        def fetch_x(b):
            wait("gpsimd", *st["xr_free"])
            st["x_in"] = [dma(lambda e: e.dma_start(xr[:, :, :], x_rows(b)), "x_in", "gpsimd")]

        proj_in = load("proj_in", (ident[:, :], t["c_ident"]),
                       (wqkv[:, :, :], t["wqkv"].rearrange("(c p) n -> p c n", p=P)),
                       (bqk[:, :, :], t["bqk"]), (bv_all[:, :], t["bv"].broadcast_to([P, D])))
        do("vector", lambda e: e.memset(minus_half[:, :], -0.5), "dve_setup")
        first_set = do("vector", lambda e: e.memset(ones_row[:, :], 1.0), "dve_setup")

        st = {"unit": 0, "side": 0, "xT_free": [], "xn_free": [], "xr_free": [], "v": {}, "split": {},
              "prob_free": [None] * NPROB, "main": {}, "spread": {}, "spread_unit": {}, "on": {},
              "av_free": None, "sc_free": [], "sent": [], "pT_free": None, "q_ready": {}, "x_in": x0_in}
        spread_next = [0]

        def side_bank():
            st["side"] += 1
            return NSCORE + st["side"] % NSIDE

        def layer_norm(tiles, *ready):
            part = slice(tiles[0], tiles[-1] + 1)
            for tt in tiles:
                wait("vector", *ready[tt // 2:tt // 2 + 1] if len(ready) > 1 else ready)
                m = do("vector", lambda e, tt=tt: e.bn_stats(stats[:, tt, :], xr[:, tt, :]), "dve_norm")
                yield
            wait("vector", m)
            for tt in tiles:
                m = do("vector", lambda e, tt=tt: e.bn_aggr(mv[:, tt, :], stats[:, tt, :]), "dve_norm")
            wait("vector", m)
            m = do("vector", lambda e: e.tensor_scalar(varp[:, part], mv[:, part, 1], EPS, None, ALU.add), "dve_norm")
            wait("gpsimd", m)
            m = do("gpsimd", lambda e: e.tensor_tensor(rstd[:, part], varp[:, part], minus_half[:, part], ALU.pow), "pool_norm")
            yield from pause(2)
            wait("vector", m)
            m = do("vector", lambda e: e.scalar_tensor_tensor(
                out=shift[:, part], in0=mv[:, part, 0], scalar=-1.0, in1=rstd[:, part], op0=ALU.mult, op1=ALU.mult), "dve_norm")
            wait("scalar", m, *ready, *st["xn_free"])
            for tt in tiles:
                m = do("scalar", lambda e, tt=tt: e.activation(
                    xn[:, tt, 0:D], xr[:, tt, :], ACT.Identity, bias=shift[:, tt:tt + 1], scale=rstd[:, tt:tt + 1]), "act_norm")
                yield
            return m

        def pause(steps):
            for _ in range(steps):
                yield

        def turn(tiles, src, ready, free):
            wait("scalar", *free)
            for c in range(DC):
                for four in range(tiles[0] // 4, (tiles[-1] + 1) // 4):
                    bank = side_bank()
                    pe_into([bank], *ready)
                    for q in range(4):
                        m = do("tensor", lambda e, c=c, tt=4 * four + q, q=q, bank=bank: e.transpose(
                            ps[:, bank, q * P:(q + 1) * P], src[:, tt, c * P:(c + 1) * P], ident[:, :]), "pe_turn")
                    wait("scalar", m)
                    made = do("scalar", lambda e, c=c, four=four, bank=bank: e.activation(
                        xT[:, c, four * BANK:(four + 1) * BANK], ps[:, bank, :], ACT.Copy), "act_turn")
                    read_by([bank], made)
                    yield
            yield
            return made, m

        def prepare(b):
            wait("gpsimd", first_set)
            normed = yield from layer_norm(range(NT), *st["x_in"])
            st["xr_free"] = [normed]
            if b:
                fetch_x(b - 1)
            wait("tensor", proj_in)
            turned, read = yield from turn(range(NT), xn, [normed], st["xT_free"])
            st["xn_free"] = [read]
            wait("tensor", turned)
            wait("scalar", proj_in)
            wait("vector", proj_in)
            while b and st["unit"] < st["spread_unit"].get(NG * b - 1, NB * S) + 20:
                yield
            for G in range(NG * (b - 1), NG * b) if b else ():
                wait("scalar", *st["spread"][G].values())
                wait("vector", *st["spread"][G].values())
            if b == 0:
                wait("vector", proj_in)
                do("vector", lambda e: e.tensor_scalar(wqkv[:, :, 0:D], wqkv[:, :, 0:D], DH ** -0.5, None, ALU.mult), "dve_setup")
                scaled = do("vector", lambda e: e.tensor_scalar(bqk[:, 0, :], bqk[:, 0, :], DH ** -0.5, None, ALU.mult), "dve_setup")
                wait("tensor", scaled)
                wait("scalar", scaled)
                wait("vector", scaled)
            for mo in range(DC):
                for a in range(2):
                    for ch in range(NCH):
                        bank = side_bank()
                        pe_into([bank])
                        for c in range(DC):
                            m = do("tensor", lambda e, a=a, mo=mo, ch=ch, c=c, bank=bank: e.matmul(
                                ps[:, bank, :], wqkv[:, c, a * D + mo * P:a * D + (mo + 1) * P],
                                xT[:, c, ch * BANK:(ch + 1) * BANK], start=(c == 0), stop=(c == DC - 1)), "pe_proj")
                        cols = slice(ch * BANK, (ch + 1) * BANK)
                        wait("scalar", m)
                        mh = do("scalar", lambda e, a=a, mo=mo, cols=cols, bank=bank: e.activation(
                            hi[a][:, mo, cols], ps[:, bank, :], ACT.Identity, bias=bqk[:, a, mo:mo + 1]), "act_high")
                        wait("vector", mh)
                        st["split"][b, mo] = ml = do("vector", lambda e, a=a, mo=mo, cols=cols, bank=bank: e.scalar_tensor_tensor(
                            out=lo[a][:, mo, cols], in0=ps[:, bank, :], scalar=bqk[:, a, mo:mo + 1],
                            in1=hi[a][:, mo, cols].bitcast(F32), op0=ALU.add, op1=ALU.subtract), "dve_low")
                        read_by([bank], ml)
                        if a == 1 and ch == NCH - 1:
                            spread_when_ready()
                        yield
            for two in range(NT // 2):
                bank = side_bank()
                pe_into([bank])
                for k in range(2):
                    for c in range(DC):
                        m = do("tensor", lambda e, tt=2 * two + k, k=k, c=c, bank=bank: e.matmul(
                            ps[:, bank, k * D:(k + 1) * D], xT[:, c, tt * P:(tt + 1) * P], wqkv[:, c, 2 * D:3 * D],
                            start=(c == 0), stop=(c == DC - 1)), "pe_proj")
                wait("vector", m, st["main"].get(NG * (b - 1) - 1), v_ones)
                for k in range(2):
                    st["v"][b] = mv_ = do("vector", lambda e, tt=2 * two + k, k=k, bank=bank: e.tensor_tensor(
                        vt[b % 2][:, tt, 0:NH * VW].rearrange("p (h d) -> p h d", h=NH)[:, :, 0:DH],
                        ps[:, bank, k * D:(k + 1) * D].rearrange("p (h d) -> p h d", h=NH),
                        bv_all[:, :].rearrange("p (h d) -> p h d", h=NH), ALU.add), "dve_v")
                read_by([bank], mv_)
                yield
            st["xT_free"] = [m]

        def zeros_and_ones():
            for i in range(2):
                do("vector", lambda e, i=i: e.memset(vt[i][:, :, :], 1.0), "dve_fill")
            m_v, m = prog.mark("dve_fill"), None
            for i in range(NSET):
                for half in range(2):
                    r = HROWS * half
                    wait("gpsimd", m)
                    m = do("gpsimd", lambda e, i=i, r=r, half=half: e.memset(
                        ka[i][r:r + HROWS, 1 - half:HG:2, :].bitcast(F32), 0.0), "pool_fill")
            wait("gpsimd", m)
            return m_v, m

        def special_rows():
            kin = load("special_in", (kraw[:, :, :], t["c_kspec"].rearrange("(a p) n -> p a n", p=P)),
                       (qraw[:, :], t["c_qspec"]), (ramp_in[:, :, :], t["c_ramps"].rearrange("a p n -> p a n")),
                       (slope_in[:, :], t["c_slopes"].broadcast_to([P, NH])))
            wait("vector", kin, proj_in)
            do("vector", lambda e: e.tensor_copy(kround[:, :, :], kraw[:, :, :]), "dve_setup")
            do("vector", lambda e: e.tensor_copy(qround[:, :], qraw[:, :]), "dve_setup")
            m = prog.mark("dve_setup")
            wait("sync", m)
            back = load("special_out",
                        (self.kspec_dram.rearrange("(a p) n -> p a n", p=P), kround[:, :, :].bitcast(F32)),
                        (self.qspec_dram, qround[:, :].bitcast(F32)))
            do("vector", lambda e: e.tensor_copy(ramps[:, :, :], ramp_in[:, :, :]), "dve_setup")
            for h in range(NH):
                m = do("vector", lambda e, h=h: e.tensor_scalar(slopes[:, h, :], ident[:, :], slope_in[:, h:h + 1], None, ALU.mult), "dve_setup")
            return back, m

        kraw = prob[:, 0:4, :].rearrange("p a n -> p (a n)").rearrange("p (a n) -> p a n", a=2)
        kround = qa[2][:, 0:2, :]
        qraw = on[0:DH, 0:4, :].rearrange("p a n -> p (a n)")
        qround = qa[1][0:DH, 0, :]
        ramp_in = on[:, 4, :].rearrange("p (a n) -> p a n", a=2)
        slope_in = sc[:, 0, 0:NH]
        opening = prepare(0)
        for _ in range(NT + 3):
            next(opening)
        v_ones, k_zeros = zeros_and_ones()
        specials, slopes_done = special_rows()

        def context_products():
            NC = NB * CTX
            w = {n: xn[:, 2 * i:2 * i + 2, 0:D]
                 for i, n in enumerate(("xwk", "xwv", "xwq"))}
            cx = xr[:, 0:NB, :]
            cT, kT, vT = (flat(xT[:, :, :])[:, n * DC * NC:(n + 1) * DC * NC].rearrange("p (c n) -> p c n", c=DC)
                          for n in range(3))
            bias = {n: sc[:, 1, 2 * i:2 * i + 2] for i, n in enumerate(("xbq", "xbk", "xbv"))}
            wait("gpsimd", slopes_done, specials, *st["xn_free"], *st["xr_free"], *st["xT_free"])
            wait("vector", *st["xT_free"])
            m_in = load("context_in", *[(w[n], t[n].rearrange("(c p) n -> p c n", p=P)) for n in w],
                        *[(bias[n], t[n]) for n in bias],
                        (cx[0:CTX, :, :], t["ctx"].rearrange("b c d -> c b d")),
                        (xwo[:, :, :], t["xwo"].rearrange("(c p) n -> p c n", p=P)), engine="gpsimd")
            yield from pause(10)
            wait("tensor", m_in)
            for c in range(DC):
                bank = side_bank()
                pe_into([bank])
                for b in range(NB):
                    m = do("tensor", lambda e, b=b, c=c, bank=bank: e.transpose(
                        ps[:, bank, b * CTX:(b + 1) * CTX], cx[0:CTX, b, c * P:(c + 1) * P], ident[0:CTX, 0:CTX]), "pe_setup")
                wait("vector", m)
                m = do("vector", lambda e, c=c, bank=bank: e.tensor_copy(cT[:, c, :], ps[:, bank, 0:NC]), "dve_setup")
                read_by([bank], m)
                yield
            wait("tensor", m)
            for name, bname, out_ in (("xwk", "xbk", kT), ("xwv", "xbv", vT)):
                for mo in range(DC):
                    bank = side_bank()
                    pe_into([bank])
                    for c in range(DC):
                        m = do("tensor", lambda e, name=name, mo=mo, c=c, bank=bank: e.matmul(
                            ps[:, bank, 0:NC], w[name][:, c, mo * P:(mo + 1) * P], cT[:, c, :],
                            start=(c == 0), stop=(c == DC - 1)), "pe_setup")
                    wait("vector", m, m_in)
                    m = do("vector", lambda e, out_=out_, mo=mo, bank=bank, bname=bname: e.tensor_scalar(
                        out_[:, mo, :], ps[:, bank, 0:NC], bias[bname][:, mo:mo + 1], None, ALU.add), "dve_setup")
                    read_by([bank], m)
                    yield
            wait("tensor", m)
            for mo in range(DC):
                bank = side_bank()
                pe_into([bank])
                for c in range(DC):
                    m = do("tensor", lambda e, mo=mo, c=c, bank=bank: e.matmul(
                        ps[:, bank, 0:NC], w["xwq"][:, c, mo * P:(mo + 1) * P], kT[:, c, :],
                        start=(c == 0), stop=(c == DC - 1)), "pe_setup")
                wait("vector", m)
                m = do("vector", lambda e, mo=mo, bank=bank: e.tensor_copy(
                    ctx_keys[:, :, mo, :], ps[:, bank, 0:NC].rearrange("p (b j) -> p b j", b=NB)), "dve_setup")
                read_by([bank], m)
                yield
            bank = side_bank()
            pe_into([bank])
            for c in range(DC):
                m = do("tensor", lambda e, c=c, bank=bank: e.matmul(
                    ps[0:1, bank, 0:NC], bias["xbq"][:, c:c + 1], kT[:, c, :], start=(c == 0), stop=(c == DC - 1)), "pe_setup")
            wait("vector", m)
            m = do("vector", lambda e, bank=bank: e.tensor_copy(ctx_bias[:, :, :].rearrange("p b j -> p (b j)"), ps[0:1, bank, 0:NC]), "dve_setup")
            read_by([bank], m)
            for b in range(NB):
                bank = side_bank()
                pe_into([bank])
                for c in range(DC):
                    m = do("tensor", lambda e, b=b, c=c, bank=bank: e.matmul(
                        ps[0:CTX, bank, 0:D], vT[:, c, b * CTX:(b + 1) * CTX], xwo[:, c, :], start=(c == 0), stop=(c == DC - 1)), "pe_setup")
                st["xn_free"] = st["xr_free"] = [m]
                wait("vector", m)
                m = do("vector", lambda e, b=b, bank=bank: e.tensor_copy(ctx_vals[:, b, :], ps[0:CTX, bank, 0:D]), "dve_setup")
                read_by([bank], m)
                yield
            st["ctx_done"] = m
            fetch_x(1)
            yield from pause(8)
            st["xT_free"] = st["xn_free"]

        def spread(G):
            b, g, i = G // NG, G % NG, G % NSET
            wait("sync", st["split"][b, g * HG // 8], st["main"].get(G - NSET), k_zeros, specials, slopes_done)
            st["spread_unit"][G] = st["unit"]
            for hh in range(HG):
                h = g * HG + hh
                mo, r = h // 8, (h % 8) * DH
                base = HROWS * (hh % 2)
                q_rows = (self.qspec_dram, hi[0][r:r + DH, mo, :].bitcast(F32), lo[0][r:r + DH, mo, :].bitcast(F32),
                          hi[0][r:r + DH, mo, :].bitcast(F32))
                k_rows = (self.kspec_dram[h * DH:(h + 1) * DH, :], hi[1][r:r + DH, mo, :].bitcast(F32),
                          hi[1][r:r + DH, mo, :].bitcast(F32), lo[1][r:r + DH, mo, :].bitcast(F32))
                for j in range(4):
                    part = slice(base + DH * j, base + DH * (j + 1))
                    load(f"spread{i}_{hh // 2}", (qa[i][part, hh // 2, :].bitcast(F32), q_rows[j]))
                    m = load(f"spread{i}_{hh // 2}", (ka[i][part, hh, :].bitcast(F32), k_rows[j]))
                st["spread"].setdefault(G, {})[hh // 2] = m

        def spread_when_ready():
            while spread_next[0] < NB * NG:
                G = spread_next[0]
                if G >= NSET and G - NSET not in st["main"] or (G // NG, G % NG * HG // 8) not in st["split"]:
                    return
                spread(G)
                spread_next[0] += 1

        def row_maxima(G):
            g, i = G % NG, G % NSET
            for hh in range(HG):
                wait("tensor", st["spread"][G][hh // 2])
                h = g * HG + hh
                for qt in range(NT):
                    for kc in range(NCH):
                        bank = side_bank()
                        pe_into([bank])
                        m = do("tensor", lambda e, hh=hh, qt=qt, kc=kc, bank=bank: e.matmul(
                            ps[:, bank, :], qa[i][:, hh // 2, qt * P:(qt + 1) * P],
                            ka[i][:, hh, kc * BANK:(kc + 1) * BANK], start=True, stop=True), "pe_max")
                        if qt // 4 == kc:
                            m = do("tensor", lambda e, h=h, bank=bank, qt=qt: e.matmul(
                                ps[:, bank, (qt % 4) * P:(qt % 4 + 1) * P], slopes[:, h, :], ramps[:, 1 - qt % 2, :],
                                start=False, stop=True, skip_group_check=True), "pe_max")
                        wait("vector", m)
                        m = do("vector", lambda e, n=hh * NT + qt, kc=kc, bank=bank: e.tensor_reduce(
                            rmax[:, n, kc:kc + 1], ps[:, bank, :], AX.X, ALU.max), "dve_max")
                        read_by([bank], m)
                        yield
            wait("vector", m)
            m = do("vector", lambda e: e.tensor_reduce(nmax[:, :], rmax[:, :, :], AX.X, ALU.max), "dve_max")
            bank = side_bank()
            pe_into([bank], m)
            m = do("tensor", lambda e, bank=bank: e.transpose(ps[0:HG * NT, bank, 0:P], nmax[:, :], ident[:, :]), "pe_max")
            wait("vector", m, st.get("nrow_free"))
            m = do("vector", lambda e, bank=bank: e.tensor_scalar(nrow[:, :], ps[0:HG * NT, bank, 0:P], -1.0, None, ALU.mult), "dve_max")
            read_by([bank], m)
            wait("sync", m)
            for hh in range(HG):
                row = HROWS * (hh % 2) + MAX_ROW
                m = load("max_rows", (qa[i][row:row + 1, hh // 2, :].bitcast(F32), nrow[hh * NT:(hh + 1) * NT, :].bitcast(F32)))
            st["nrow_free"] = st["q_ready"][G] = m
            yield

        def main_pass(G, between):
            b, g, i = G // NG, G % NG, G % NSET
            wait("tensor", st["q_ready"][G], st["v"][b], slopes_done)

            def scores(ch, kt, hh):
                bank, slot = st["unit"] % NSCORE, st["unit"] % NPROB
                st["unit"] += 1
                pe_into([bank])
                m = do("tensor", lambda e: e.matmul(
                    ps[:, bank, :], ka[i][:, hh, kt * P:(kt + 1) * P],
                    qa[i][:, hh // 2, ch * BANK:(ch + 1) * BANK], start=True, stop=True), "pe_scores")
                if kt // 4 == ch:
                    m = do("tensor", lambda e: e.matmul(
                        ps[:, bank, (kt % 4) * P:(kt % 4 + 1) * P], slopes[:, g * HG + hh, :], ramps[:, kt % 2, :],
                        start=False, stop=True, skip_group_check=True), "pe_scores")
                return bank, slot, m

            def exp(bank, slot, m):
                wait("scalar", m, st["prob_free"][slot])
                m = do("scalar", lambda e: e.activation(prob[:, slot, :], ps[:, bank, :], ACT.Exp), "act_prob")
                read_by([bank], m)
                return slot, m

            def attend(ch, kt, made):
                bank = 6 + ch
                if kt == 0:
                    pe_into([bank])
                wait("tensor", made[-1][1])
                for hh, (slot, _) in enumerate(made):
                    c0 = (g * HG + hh) * VW
                    m = do("tensor", lambda e, hh=hh, c0=c0, slot=slot: e.matmul(
                        ps[CT * hh:CT * (hh + 1), bank, :], vt[b % 2][:, kt, c0:c0 + CT], prob[:, slot, :],
                        start=(kt == 0), stop=(kt == NT - 1)), "pe_attend")
                for slot, _ in made:
                    st["prob_free"][slot] = m
                return m

            def finish(ch, m):
                bank = 6 + ch
                wait("scalar", m, st["av_free"])
                m = do("scalar", lambda e: e.activation(av[:, :], ps[:, bank, :], ACT.Copy), "act_av")
                read_by([bank], m)
                yield
                pe_into([bank], m)
                for q in range(4):
                    m = do("tensor", lambda e, q=q: e.transpose(
                        ps[:, bank, q * P:(q + 1) * P], av[:, q * P:(q + 1) * P], ident[:, :]), "pe_av")
                st["av_free"] = m
                yield
                wait("vector", m, *(st.get("on_free", []) if g == 0 else []))
                heads = ps[:, bank, :].rearrange("p (n c) -> p n c", c=CT)
                m = do("vector", lambda e: e.reciprocal(rden[:, :], heads[:, :, DH]), "dve_on")
                wait("vector", m)
                m = do("vector", lambda e: e.tensor_tensor(
                    on[:, 4 * ch:4 * ch + 4, g * HG * DH:(g + 1) * HG * DH].rearrange("p t (h d) -> p t h d", h=HG),
                    heads[:, :, 0:DH].rearrange("p (t h) d -> p t h d", h=HG),
                    rden[:, :].rearrange("p (t h) -> p t h", h=HG).unsqueeze(3).broadcast_to([P, 4, HG, DH]), ALU.mult), "dve_on")
                read_by([bank], m)
                wait("vector", m)
                st["on"][G, ch] = m

            waiting, closing = [], []

            def close_one():
                if closing and next(closing[0], "end") == "end":
                    closing.pop(0)

            for ch in range(NCH):
                for kt in range(NT):
                    made = [exp(*scores(ch, kt, 0))]
                    between(3)
                    made.append(exp(*scores(ch, kt, 1)))
                    between(0)
                    third = scores(ch, kt, 2) if G == NB * NG - 1 else None
                    if waiting:
                        c_, k_, made_ = waiting.pop(0)
                        m = attend(c_, k_, made_)
                        if k_ == NT - 1:
                            closing.append(finish(c_, m))
                            close_one()
                    between(1)
                    made.append(exp(*(third or scores(ch, kt, 2))))
                    between(4)
                    made.append(exp(*scores(ch, kt, 3)))
                    waiting.append((ch, kt, made))
                    between(2)
                    close_one()
            c_, k_, made_ = waiting.pop(0)
            st["main"][G] = m = attend(c_, k_, made_)
            closing.append(finish(c_, m))
            return closing

        def complete(b, chunks, pT):
            tiles = range(4 * chunks[0], 4 * chunks[-1] + 4)
            part = slice(tiles[0], tiles[-1] + 1)
            xn_free = st["xn_free"]
            wait("gpsimd", *st["x_in"], late_in)
            for tt in tiles:
                xo = do("gpsimd", lambda e, tt=tt: e.tensor_tensor(xr[:, tt, :], xr[:, tt, :], bo_all[:, :], ALU.add), "pool_bias")
            yield from pause(4)
            turned, on_read = yield from turn(tiles, on, [st["on"][NG * b + NG - 1, ch] for ch in chunks], st["xT_free"])
            st["on_free"] = [on_read]
            wait("tensor", turned, late_in)
            wait("vector", xo)

            def add_rows(two, m, bank):
                wait("vector", m)
                m = do("vector", lambda e: e.tensor_tensor(
                    flat(xr[:, 2 * two:2 * two + 2, :]), ps[:, bank, :], flat(xr[:, 2 * two:2 * two + 2, :]), ALU.add), "dve_rows")
                read_by([bank], m)
                return m

            for two in range(tiles[0] // 2, tiles[-1] // 2 + 1):
                bank = side_bank()
                pe_into([bank])
                for k in range(2):
                    for c in range(DC):
                        m = do("tensor", lambda e, tt=2 * two + k, k=k, c=c, bank=bank: e.matmul(
                            ps[:, bank, k * D:(k + 1) * D], xT[:, c, tt * P:(tt + 1) * P], wo[:, c, :],
                            start=(c == 0), stop=(c == DC - 1)), "pe_out")
                x1 = add_rows(two, m, bank)
                yield
            xT_free = [m]
            normed = yield from layer_norm(tiles, x1)
            wait("gpsimd", normed)
            for tt in tiles:
                xo = do("gpsimd", lambda e, tt=tt: e.tensor_tensor(xr[:, tt, :], xr[:, tt, :], xbo_all[:, :], ALU.add), "pool_bias")
            turned, read = yield from turn(tiles, xn, [normed], xT_free)
            st["xn_free"] = st["xn_free"] + [read]
            wait("tensor", turned, st["ctx_done"])
            for four in chunks:
                bank = side_bank()
                pe_into([bank])
                for q in range(4):
                    cols = slice(q * CTX, (q + 1) * CTX)
                    for c in range(DC):
                        do("tensor", lambda e, tt=4 * four + q, c=c, bank=bank, cols=cols: e.matmul(
                            ps[:, bank, cols], xT[:, c, tt * P:(tt + 1) * P], ctx_keys[:, b, c, :], start=(c == 0), stop=False))
                    m = do("tensor", lambda e, bank=bank, cols=cols: e.matmul(
                        ps[:, bank, cols], ones_row[:, :], ctx_bias[:, b, :], start=False, stop=True), "pe_ctx")
                wait("vector", m, *st["sc_free"])
                fours = slice(4 * four, 4 * four + 4)
                scv = ps[:, bank, 0:4 * CTX].rearrange("p (t j) -> p t j", t=4)
                m = do("vector", lambda e, fours=fours, scv=scv: e.tensor_reduce(smax[:, fours], scv, AX.X, ALU.max), "dve_ctx")
                wait("vector", m)
                m = do("vector", lambda e, fours=fours, scv=scv: e.tensor_tensor(
                    sc[:, fours, :], scv, smax[:, fours].unsqueeze(2).broadcast_to([P, 4, CTX]), ALU.subtract), "dve_ctx")
                read_by([bank], m)
                yield
            wait("scalar", m)
            m = do("scalar", lambda e: e.activation(sc[:, part, :], sc[:, part, :], ACT.Exp, scale=D ** -0.5), "act_ctx")
            yield from pause(2)
            wait("vector", m)
            m = do("vector", lambda e: e.tensor_reduce(ssum[:, part], sc[:, part, :], AX.X, ALU.add), "dve_ctx")
            wait("vector", m)
            m = do("vector", lambda e: e.reciprocal(smax[:, part], ssum[:, part]), "dve_ctx")
            wait("vector", m)
            m = do("vector", lambda e: e.tensor_tensor(sc[:, part, :], sc[:, part, :], smax[:, part].unsqueeze(2).broadcast_to([P, len(tiles), CTX]), ALU.mult), "dve_ctx")
            yield from pause(2)
            wait("vector", xo)
            sc_ready, pT_free = m, st["pT_free"]
            for two in range(tiles[0] // 2, tiles[-1] // 2 + 1):
                if two % 2 == 0:
                    bank = side_bank()
                    pe_into([bank], sc_ready)
                    for q in range(4):
                        m = do("tensor", lambda e, tt=2 * two + q, q=q, bank=bank: e.transpose(
                            ps[0:CTX, bank, q * P:(q + 1) * P], sc[:, tt, :], ident[:, :]), "pe_ctx")
                    sc_free = m
                    wait("scalar", m, pT_free)
                    mp = do("scalar", lambda e, bank=bank: e.activation(pT[:, :], ps[0:CTX, bank, :], ACT.Copy), "act_ctx")
                    read_by([bank], mp)
                    yield from pause(2)
                    wait("tensor", mp)
                bank = side_bank()
                pe_into([bank])
                for k in range(2):
                    for c in range(DC):
                        do("tensor", lambda e, tt=2 * two + k, k=k, c=c, bank=bank: e.matmul(
                            ps[:, bank, k * D:(k + 1) * D], xT[:, c, tt * P:(tt + 1) * P], xwo[:, c, :], start=(c == 0), stop=False))
                    m = do("tensor", lambda e, at=(2 * two + k) % 4, k=k, bank=bank: e.matmul(
                        ps[:, bank, k * D:(k + 1) * D], pT[:, at * P:(at + 1) * P], ctx_vals[:, b, :], start=False, stop=True), "pe_out")
                pT_free = m
                x2 = add_rows(two, m, bank)
                yield
            st["pT_free"], st["sc_free"] = pT_free, st["sc_free"] + [sc_free]
            xT_free = [m]
            wait("sync", x2)
            stored = load("x2_out", (t["out"][b * S:(b + 1) * S, :].rearrange("(t p) d -> p t d", p=P)[:, part, :], xr[:, part, :]))
            normed = yield from layer_norm(tiles, x2)
            st["xr_free"] = [normed, stored]
            if b + 1 < NB:
                fetch_x(min(b + 2, NB - 1))
            turned, read = yield from turn(tiles, xn, [normed], xT_free)
            wait("tensor", turned)
            bank = side_bank()
            pe_into([bank])
            for tt in tiles:
                for c in range(DC):
                    m = do("tensor", lambda e, tt=tt, c=c, bank=bank: e.matmul(
                        ps[:, bank, tt * NE:(tt + 1) * NE], xT[:, c, tt * P:(tt + 1) * P], wr[:, c, :],
                        start=(c == 0), stop=(c == DC - 1)), "pe_out")
            st["xT_free"] = [m]
            yield from route(b, tiles, bank, m)
            st["xn_free"] = xn_free + [read, self.scattered]

        def route(b, tiles, bank, logits_made):
            wait("vector", logits_made, late_in, route_in)

            def v(step):
                m = do("vector", step, "dve_route")
                wait("vector", m)
                return m

            part, n = slice(tiles[0], tiles[-1] + 1), len(tiles)
            cols = slice(tiles[0] * NE, (tiles[-1] + 1) * NE)
            bc = lambda a: a.unsqueeze(2).broadcast_to([P, n, NE])
            be = lambda a: a.unsqueeze(1).broadcast_to([P, n, NE])
            three = lambda a: a.rearrange("p (t n) -> p t n", n=NE)
            m = v(lambda e, bank=bank: e.tensor_tensor(logits[:, part, :], three(ps[:, bank, cols]), be(br_all[:, :]), ALU.add))
            read_by([bank], m)
            src = logits
            for k in range(TOPK):
                v(lambda e, k=k, src=src: e.tensor_reduce(top[k][:, part], src[:, part, :], AX.X, ALU.max))
                v(lambda e, k=k, src=src: e.tensor_tensor(tmp[:, part, :], src[:, part, :], bc(top[k][:, part]), ALU.is_equal))
                v(lambda e: e.tensor_tensor(tmp[:, part, :], tmp[:, part, :], be(pick_order[:, :]), ALU.mult))
                v(lambda e: e.tensor_reduce(first[:, part], tmp[:, part, :], AX.X, ALU.max))
                v(lambda e, k=k: e.tensor_tensor(chosen[k][:, part, :], bc(first[:, part]), be(pick_order[:, :]), ALU.is_equal))
                if k == 0:
                    v(lambda e: e.tensor_copy(code[:, part], first[:, part]))
                    v(lambda e: e.scalar_tensor_tensor(out=flat(rest[:, part, :]), in0=flat(chosen[0][:, part, :]), scalar=-3.0e38,
                                                       in1=flat(logits[:, part, :]), op0=ALU.mult, op1=ALU.add))
                    yield
                src = rest
            yield
            m = v(lambda e: e.tensor_tensor(wt[:, part], top[1][:, part], top[0][:, part], ALU.subtract))
            wait("scalar", m)
            exped = do("scalar", lambda e: e.activation(wt[:, part], wt[:, part], ACT.Exp), "act_route")
            m = v(lambda e: e.tensor_tensor(tmp[:, part, :], chosen[0][:, part, :], chosen[1][:, part, :], ALU.add))
            yield from pause(2)
            bank = side_bank()
            pe_into([bank], m)
            do("tensor", lambda e, bank=bank: e.matmul(ps[:, bank, 0:n * NE], earlier[:, :], flat(tmp[:, part, :]), start=True, stop=True))
            m = do("tensor", lambda e, bank=bank: e.matmul(ps[:, bank, n * NE:2 * n * NE], every[:, :], flat(tmp[:, part, :]), start=True, stop=True), "pe_route")
            wait("vector", m, exped)
            in_all = slice(b * NT + tiles[0], b * NT + tiles[-1] + 1)
            v(lambda e: e.tensor_copy(upto[:, tiles[0], :], count[:, :]))
            for tt in tiles:
                v(lambda e, tt=tt, bank=bank: e.tensor_tensor(
                    upto[:, tt + 1, :], ps[:, bank, (n + tt - tiles[0]) * NE:(n + tt - tiles[0] + 1) * NE], upto[:, tt, :], ALU.add))
            m = v(lambda e, bank=bank: e.tensor_tensor(place[:, part, :], three(ps[:, bank, 0:n * NE]), upto[:, part, :], ALU.add))
            read_by([bank], m)
            v(lambda e: e.tensor_copy(count[:, :], upto[:, tiles[-1] + 1, :]))
            yield
            v(lambda e: e.tensor_tensor(place[:, part, :], place[:, part, :], be(region[:, :]), ALU.add))
            for k in range(TOPK):
                v(lambda e, k=k: e.tensor_tensor(tmp[:, part, :], place[:, part, :], chosen[k][:, part, :], ALU.mult))
                v(lambda e: e.tensor_reduce(slotf[:, part], tmp[:, part, :], AX.X, ALU.add))
                slots = v(lambda e, k=k: e.tensor_copy(self.slot[k][:, in_all], slotf[:, part]))
            yield
            v(lambda e: e.tensor_scalar(first[:, part], wt[:, part], 1.0, None, ALU.add))
            v(lambda e: e.reciprocal(top[0][:, part], first[:, part]))
            v(lambda e: e.tensor_tensor(top[1][:, part], top[0][:, part], wt[:, part], ALU.mult))
            wait("vector", *st["sent"])
            v(lambda e: e.tensor_copy(xn[:, part, CODE], code[:, part]))
            v(lambda e: e.tensor_scalar(xn[:, part, TOKEN].bitcast(I32), self.steps[:, in_all], self.steps[:, P - 1:P], None, ALU.add))
            v(lambda e: e.tensor_copy(xn[:, part, SECOND], top[1][:, part]))
            st["routed"] = slots = v(lambda e: e.tensor_tensor(xn[:, part, MORE], top[0][:, part], top[1][:, part], ALU.subtract))
            yield
            if tiles[-1] < NT - 1:
                yield from pause(14)
            wait("gpsimd", slots)
            for tt in tiles:
                for k in range(TOPK):
                    self.scattered = dma(lambda e, tt=tt, k=k: e.indirect_dma_start(
                        self.rows_in, bass.IndirectOffsetOnAxis(ap=self.slot[k][:, b * NT + tt:b * NT + tt + 1], axis=0),
                        xn[:, tt, :], None), "scattered", "gpsimd")
                if tt % 4 == 3:
                    yield
            if tiles[-1] == NT - 1:
                st["sent"] = [self.scattered]
            yield from pause(22)

        def background():
            for b in range(NB):
                if b:
                    yield from complete(b - 1, range(NCH), pT)
                if b + 1 < NB:
                    yield from prepare(b + 1)
                if b == NB - 1:
                    while (NB * NG - 1, 0) not in st["on"]:
                        yield
                    yield from complete(b, [0], pT)
                while len(st["main"]) < NG * (b + 1):
                    yield

        for _ in opening:
            pass
        back = chain(context_products(), background())
        next(back)
        late_in = load("late_in", (wo[:, :, :], t["wo"].rearrange("(c p) n -> p c n", p=P)),
                       (bo_all[:, :], t["bo"].broadcast_to([P, D])), (xbo_all[:, :], t["xbo"].broadcast_to([P, D])),
                       (wr[:, :, :], t["wr"].rearrange("(c p) n -> p c n", p=P)), (br_all[:, :], t["br"].broadcast_to([P, NE])),
                       (earlier[:, :], t["c_low"]), (self.steps[:, :], t["c_first"]))
        wait("vector", slopes_done)
        wait("tensor", slopes_done)
        for i, _ in enumerate(row_maxima(0)):
            if i % 2:
                next(back)
        wait("vector", late_in)
        do("vector", lambda e: e.memset(every[:, :], 1.0), "dve_setup")
        do("vector", lambda e: e.memset(count[:, :], 0.0), "dve_setup")
        do("vector", lambda e: e.memset(self.no_rows[:, 0:D], 0.0), "dve_setup")
        do("vector", lambda e: e.memset(self.no_rows[:, CODE:SENT], 0.0), "dve_setup")
        zeroed = do("vector", lambda e: e.tensor_scalar(
            self.no_rows[:, TOKEN:TOKEN + 1].bitcast(I32), self.steps[:, P - 1:P], float(TOK), None, ALU.add), "dve_setup")
        do("vector", lambda e: e.tensor_scalar(pick_order[:, :], self.steps[:, 0:NE], -1.0 / P, float(NE), ALU.mult, ALU.add), "dve_setup")
        route_in = do("vector", lambda e: e.tensor_scalar(region[:, :], self.steps[:, 0:NE], float(REGION // P), None, ALU.mult), "dve_setup")
        wait("sync", zeroed)
        for n in range(NIDLE):
            self.idle_zeroed = load("idle_zeroed", (self.rows_in[NE * REGION + n * P:NE * REGION + (n + 1) * P, :], self.no_rows[:, :]))
        self.idle_zeroed = load("idle_zeroed", (t["out"][TOK:TOK + P, :], self.no_rows[:, 0:D]))

        closing = []
        for G in range(NB * NG):
            maxima = row_maxima(G + 1) if G + 1 < NB * NG else iter(())
            places = [0, 0]

            def between(where):
                nonlocal closing
                places[0] += 1
                if places[0] * (HG * NT * NCH) > places[1] * MAXIMA_END:
                    places[1] += 1
                    next(maxima, None)
                if closing and next(closing[0], "end") == "end":
                    closing.pop(0)
                if where in (1, 2, 3):
                    next(back, None)

            closing = main_pass(G, between)
            for _ in maxima:
                pass
            spread_when_ready()
            if G < NB * NG - 1:
                self.prefetch(G, st)
        for c in closing:
            for _ in c:
                pass
        self.prefetch(NB * NG - 1, st)
        wait("scalar", st["av_free"])
        parts = [back, complete(NB - 1, [1], av[0:CTX, :])]
        while parts:
            parts = [p for p in parts if next(p, "end") != "end"]

        idle = on[:, :, :].rearrange("p t d -> p (t d)")
        past = idle[:, 0:NBLK * NE].rearrange("p (b n) -> p b n", n=NE)
        past_blocks = idle[:, NBLK * NE:2 * NBLK * NE].rearrange("p (b n) -> p b n", n=NE)
        blocks_gt = idle[:, 2 * NBLK * NE:2 * NBLK * NE + NE * NTT].rearrange("p (n b) -> p n b", n=NE)
        nblocks, end, zrow = sb("nblocks", [P, NE]), sb("end", [P, NE + 1]), sb("zrow", [P, NE], I32)
        used = 2 * NBLK * NE + NE * NTT
        ended, row = (idle[:, used + i * NBLK:used + (i + 1) * NBLK] for i in range(2))

        def v(step):
            m = do("vector", step, "dve_route")
            wait("vector", m)
            return m

        zero_at = v(lambda e: e.tensor_tensor(zrow[:, :], count[:, :], region[:, :], ALU.add))
        wait("sync", zero_at)
        for n in range(NE):
            self.idle_zeroed = dma(lambda e, n=n: e.dma_start(
                self.rows_in[bass.ds(read_value(e, zrow, n, NROW - P), P), :], self.no_rows[:, :]), "idle_zeroed")
        v(lambda e: e.tensor_tensor(blocks_gt[:, :, :], count[:, :].unsqueeze(2).broadcast_to([P, NE, NTT]),
                                    self.steps[:, 0:NTT].unsqueeze(1).broadcast_to([P, NE, NTT]), ALU.is_gt))
        v(lambda e: e.tensor_reduce(nblocks[:, :], blocks_gt[:, :, :], AX.X, ALU.add))
        v(lambda e: e.memset(end[:, 0:1], 0.0))
        for n in range(NE):
            v(lambda e, n=n: e.tensor_tensor(end[:, n + 1:n + 2], end[:, n:n + 1], nblocks[:, n:n + 1], ALU.add))
        v(lambda e: e.tensor_scalar(row[:, :], self.steps[:, 0:NBLK], 1.0 / P, None, ALU.mult))
        v(lambda e: e.tensor_tensor(past[:, :, :], row[:, :].unsqueeze(2).broadcast_to([P, NBLK, NE]),
                                    end[:, 1:NE + 1].unsqueeze(1).broadcast_to([P, NBLK, NE]), ALU.is_ge))
        v(lambda e: e.tensor_reduce(ended[:, :], past[:, :, :], AX.X, ALU.add))
        v(lambda e: e.tensor_tensor(past_blocks[:, :, :], past[:, :, :], nblocks[:, :].unsqueeze(1).broadcast_to([P, NBLK, NE]), ALU.mult))
        v(lambda e: e.tensor_reduce(row[:, :], past_blocks[:, :, :], AX.X, ALU.add))
        v(lambda e: e.tensor_scalar(row[:, :], row[:, :], -float(P), None, ALU.mult))
        v(lambda e: e.tensor_tensor(row[:, :], row[:, :], self.steps[:, 0:NBLK], ALU.add))
        v(lambda e: e.scalar_tensor_tensor(out=self.row_of[:, :], in0=ended[:, :], scalar=float(REGION), in1=row[:, :], op0=ALU.mult, op1=ALU.add))
        self.blocks_known = v(lambda e: e.tensor_scalar(self.expert_of[:, :], ended[:, :], float(NE - 1), None, ALU.min))
        self.blocks_known = v(lambda e: e.tensor_scalar(self.code_of[:, :], self.expert_of[:, :], -1.0, float(NE), ALU.mult, ALU.add))
        self.attention_end = [st["routed"], self.scattered, self.idle_zeroed, st["main"][NB * NG - 1],
                              st["xr_free"][1], *st["x_in"], self.blocks_known]

    def prefetch(self, G, st):
        last = NB * NG - 1
        parts = {last - 3: [("w1", n) for n in range(5)], last - 2: [("w1", n) for n in range(5, 8)],
                 last - 1: [("w2", n) for n in range(3)], last: [("w2", n) for n in range(3, 8)]}.get(G, [])
        if G == last:
            parts += [("b1", None), ("b2", None)]
        if parts:
            for made in range(last - NG + 1, last + 1):
                self.prog.wait("sync", *st["spread"][made].values())
            self.prog.wait("sync", st["main"][G])
        for name, n in parts:
            if n is not None:
                step = lambda e, name=name, n=n: e.dma_start(
                    self.w[name][:, n, :, :], self.t[name][n].rearrange("(c p) f -> p c f", p=P))
            elif name == "b1":
                step = lambda e: e.dma_start(self.w["b1"][:, :, :], self.t["b1"])
            else:
                step = lambda e: e.dma_start(
                    self.w["b2"][:, :, :].rearrange("p n f -> p (n f)"), self.t["b2"].broadcast_to([P, NE * D]))
            self.weights_in = self.dma(step, "experts_in")

    def experts(self, stack):
        nc, t, prog, ps, ident, dma, pe_into, read_by = (
            self.nc, self.t, self.prog, self.ps, self.ident, self.dma, self.pe_into, self.read_by)
        do, wait = prog.do, prog.wait
        alloc = lambda stack, name, shape, dt=F32: stack.enter_context(nc.sbuf_tensor(name, shape, dt))
        w1 = alloc(stack, "w1", [P, NE, DC, FF])
        w2 = alloc(stack, "w2", [P, NE, FC, D])
        b1 = alloc(stack, "b1", [P, NE, FC])
        b2_all = alloc(stack, "b2_all", [P, NE, D])
        self.w = {"w1": w1, "w2": w2, "b1": b1, "b2": b2_all}
        experts_in = self.weights_in
        wait("sync", *self.attention_end)
        DVE_PART = 3 * FC // 4
        NX, NY = 4, 2
        sb = lambda name, shape, dt=F32: alloc(stack, name, shape, dt)
        xi = [sb(f"xi{i}", [P, SENT]) for i in range(NX)]
        xiT = [sb(f"xiT{i}", [P, DC, P]) for i in range(2)]
        hidT = [sb(f"hidT{i}", [P, FC, P]) for i in range(2)]
        w1_now = [sb(f"w1_now{i}", [P, DC, FF]) for i in range(2)]
        w2_high = [sb(f"w2_high{i}", [P, FC, D], F32R) for i in range(2)]
        w2_low = sb("w2_low", [P, FC, D], F32R)
        hid_high, hid_low = (sb(f"hid_{a}", [P, FC, P], F32R) for a in ("high", "low"))
        yo = [sb(f"yo{i}", [P, D]) for i in range(NY)]
        weight = [sb(f"weight{i}", [P, 1]) for i in range(NY)]
        bias = [sb(f"bias{i}", [P, D]) for i in range(NY)]
        wait("tensor", self.blocks_known, experts_in)
        wait("vector", *self.attention_end, experts_in)
        wait("gpsimd", *self.attention_end)
        wait("scalar", *self.attention_end, experts_in)
        regs = {}
        rd = {}

        def load_block(n):
            wait("sync", rd.get(("xi", n - NX)), rd.get(("out", n - NX)))
            rd["in", n] = dma(lambda e, n=n: e.dma_start(
                xi[n % NX][:, :], self.rows_in[bass.ds(read_value(e, self.row_of, n, NROW - P), P), :]), f"slots_in{n % NX}")

        def turn_block(n):
            pe_into([0], rd["in", n])
            for c in range(DC):
                m = do("tensor", lambda e, n=n, c=c: e.transpose(ps[:, 0, c * P:(c + 1) * P], xi[n % NX][:, c * P:(c + 1) * P], ident[:, :]), "pe_x")
            rd["xi", n] = m
            wait("scalar", m, rd.get(("up", n - 2)))
            rd["xiT", n] = m = do("scalar", lambda e, n=n: e.activation(xiT[n % 2][:, :, :].rearrange("p c n -> p (c n)"), ps[:, 0, 0:D], ACT.Copy), "act_x")
            read_by([0], m)

        def pick_weights(n):
            for engine in ("tensor", "scalar", "vector", "gpsimd"):
                do(engine, lambda e, n=n: regs.__setitem__((e.engine, n), read_value(e, self.expert_of, n, NE - 1)))
            def step(e, n=n, c=0):
                into, from_ = w1_now[n % 2][:, c, :], w1[:, bass.ds(regs[e.engine, n], 1), c, :].rearrange("p a f -> p (a f)")
                return e.activation(into, from_, ACT.Copy) if c == 0 else e.tensor_copy(into, from_)
            for c, engine in enumerate(("scalar", "vector")):
                wait(engine, rd.get(("up", n - 2)))
                rd["w1", n, c] = do(engine, lambda e, n=n, c=c: step(e, n, c), f"{engine}_weights")

        def second_weights(e, n, part):
            return w2[:, bass.ds(regs[e.engine, n], 1), part, :].rearrange("p a c f -> p (a c) f")

        def split_weights_high(n):
            wait("scalar", rd.get(("down", n - 2)))
            high = do("scalar", lambda e: e.activation(w2_high[n % 2][:, :, :], second_weights(e, n, slice(0, FC)), ACT.Copy), "scalar_split")
            rd["w2", n] = [high]

        def split_weights_low(n):
            high = rd["w2", n][0]
            for engine, part in (("vector", slice(0, DVE_PART)), ("gpsimd", slice(DVE_PART, FC))):
                wait(engine, high, rd.get(("down", n - 1)))
                rd["w2", n].append(do(engine, lambda e, part=part: e.tensor_tensor(
                    w2_low[:, part, :], second_weights(e, n, part), w2_high[n % 2][:, part, :].bitcast(F32), ALU.subtract), f"{engine}_split"))

        def up(n):
            for half, engine in enumerate(("scalar", "vector")):
                bank = 1 + 2 * (n % 2) + half
                pe_into([bank], rd["xiT", n], rd["w1", n, 0], rd["w1", n, 1])
                for q in range(FC // 2):
                    f = half * FC // 2 + q
                    for c in range(DC):
                        m = do("tensor", lambda e, n=n, c=c, bank=bank, f=f, q=q: e.matmul(
                            ps[:, bank, q * P:(q + 1) * P], w1_now[n % 2][:, c, f * P:(f + 1) * P],
                            xiT[n % 2][:, c, :], start=(c == 0), stop=(c == DC - 1)), "pe_up")
                rd["up", n] = m
                wait(engine, m, rd.get(("split", n - 2)))
                for q in range(FC // 2):
                    f = half * FC // 2 + q
                    def step(e, n=n, bank=bank, f=f, q=q, half=half):
                        into, made = hidT[n % 2][:, f, :], ps[:, bank, q * P:(q + 1) * P]
                        bias = b1[:, bass.ds(regs[e.engine, n], 1), f]
                        if half == 0:
                            return e.activation(into, made, ACT.Relu, bias=bias)
                        return e.tensor_scalar(into, made, bias, 0.0, ALU.add, ALU.max)
                    m = do(engine, step, f"{engine}_hidden")
                rd["hidT", n, half] = m
                read_by([bank], m)

        def split_hidden(n):
            wait("scalar", rd["hidT", n, 1], rd["hidT", n, 0], rd.get(("down", n - 1)))
            m = do("scalar", lambda e: e.activation(hid_high[:, :, :], hidT[n % 2][:, :, :], ACT.Copy), "scalar_hidden_high")
            wait("vector", m, rd.get(("down", n - 1)))
            rd["split", n] = do("vector", lambda e: e.tensor_tensor(
                hid_low[:, :, :], hidT[n % 2][:, :, :], hid_high[:, :, :].bitcast(F32), ALU.subtract), "vector_hidden_low")

        def down(n):
            bank = 5 + n % 2
            pe_into([bank], *rd["w2", n], rd["split", n])
            products = ((hid_high, w2_high[n % 2]), (hid_high, w2_low), (hid_low, w2_high[n % 2]))
            for c in range(FC):
                for i, (h, w) in enumerate(products):
                    m = do("tensor", lambda e, c=c, i=i, h=h, w=w: e.matmul(
                        ps[:, bank, 0:D], h[:, c, :], w[:, c, :], start=(c == 0 and i == 0), stop=(c == FC - 1 and i == 2)), "pe_down")
            rd["down", n] = m
            y, w, bw, x = yo[n % NY], weight[n % NY], bias[n % NY], xi[n % NX]
            wait("vector", rd["in", n], rd.get(("out", n - NY)))
            mw = do("vector", lambda e: e.scalar_tensor_tensor(
                out=w[:, :], in0=x[:, CODE:CODE + 1], scalar=self.code_of[:, n:n + 1], in1=x[:, MORE:MORE + 1], op0=ALU.is_equal, op1=ALU.mult), "dve_down")
            wait("vector", mw)
            mw = do("vector", lambda e: e.tensor_tensor(w[:, :], w[:, :], x[:, SECOND:SECOND + 1], ALU.add), "dve_down")
            wait("vector", mw)
            mw = do("vector", lambda e: e.tensor_scalar(
                bw[:, :], b2_all[:, bass.ds(regs[e.engine, n], 1), :].rearrange("p a f -> p (a f)"), w[:, :], None, ALU.mult), "dve_down")
            wait("vector", m, mw)
            m = do("vector", lambda e: e.scalar_tensor_tensor(
                out=y[:, :], in0=ps[:, bank, 0:D], scalar=w[:, :], in1=bw[:, :], op0=ALU.mult, op1=ALU.add), "dve_down")
            read_by([bank], m)
            wait("gpsimd", m, rd.get(("out", n - 1)))
            rd["out", n] = dma(lambda e: e.indirect_dma_start(
                t["out"], bass.IndirectOffsetOnAxis(ap=x[:, TOKEN:TOKEN + 1].bitcast(I32), axis=0),
                y[:, :], None, compute_op=ALU.add), "added", "gpsimd")

        for n in range(min(NX, NBLK)):
            load_block(n)
        turn_block(0)
        turn_block(1)
        pick_weights(0)
        pick_weights(1)
        split_weights_high(0)
        up(0)
        split_weights_low(0)
        for n in range(NBLK):
            split_hidden(n)
            if n + 1 < NBLK:
                split_weights_high(n + 1)
                up(n + 1)
            if n + 2 < NBLK:
                turn_block(n + 2)
                pick_weights(n + 2)
            down(n)
            if n + 1 < NBLK:
                split_weights_low(n + 1)
            if n + NX < NBLK:
                load_block(n + NX)

        wait("gpsimd", rd["out", NBLK - 1])


def read_value(e, table, n, most):
    return e.value_load(table[0:1, n:n + 1], min_val=0, max_val=most)


def constants():
    slopes = 0.5 ** np.arange(NH)
    pos = np.arange(S)
    tile = pos // P
    kspec = np.zeros((NH, DH, S), np.float32)
    qspec = np.zeros((DH, S), np.float32)
    for c in range(NSUB):
        sign = np.where(tile <= 2 * c, 1.0, -1.0)
        inside = (tile // 2 == c).astype(np.float32)
        kspec[:, 2 * c, :] = slopes[:, None] * (sign * pos)[None, :]
        kspec[:, 2 * c + 1, :] = -slopes[:, None] * sign[None, :]
        qspec[2 * c], qspec[2 * c + 1] = inside, pos * inside
    kspec[:, MAX_ROW, :] = 1.0
    p, f = np.arange(P)[:, None], np.arange(P)[None, :]
    ramps = np.stack([-2.0 * np.maximum(0, p - f), -2.0 * np.maximum(0, f - p)]) / 16.0
    first = np.tile(np.arange(P, dtype=np.float32)[None, :] * P, (P, 1))
    first[:, P - 1] = np.arange(P)
    return {
        "c_ident": np.eye(P, dtype=np.float32),
        "c_kspec": kspec.reshape(NH * DH, S),
        "c_slopes": (16.0 * slopes).astype(np.float32)[None, :],
        "c_ramps": ramps.astype(np.float32),
        "c_qspec": qspec,
        "c_low": (np.arange(P)[:, None] < np.arange(P)[None, :]).astype(np.float32),
        "c_first": first,
    }


def kernel(**inputs):
    import concourse.bacc as bacc
    from concourse.bass_utils import run_bass_kernel_spmd

    a = {k: np.asarray(v) for k, v in inputs.items()}
    qkv = a["L0_attn_qkv_w"].reshape(NH, 3, DH, D).transpose(3, 1, 0, 2).reshape(D, 3 * D)
    qkv_b = a["L0_attn_qkv_b"].reshape(NH, 3, DH).transpose(1, 0, 2).reshape(3, D)
    row = lambda v: v.reshape(1, -1)
    col = lambda v: v.reshape(DC, P).T
    arrays = {
        "x": a["x"], "ctx": a["ctx_1024"],
        "wqkv": qkv, "bqk": qkv_b[0:2].reshape(2, DC, P).transpose(2, 0, 1), "bv": qkv_b[2:3],
        "wo": a["L0_attn_out_w"].T, "bo": row(a["L0_attn_out_b"]),
        "xwo": a["L0_xattn_Wo"].T, "xbo": row(a["L0_xattn_bo"]),
        "xwq": a["L0_xattn_Wq"], "xwk": a["L0_xattn_Wk"].T, "xwv": a["L0_xattn_Wv"].T,
        "xbq": col(a["L0_xattn_bq"]), "xbk": col(a["L0_xattn_bk"]), "xbv": col(a["L0_xattn_bv"]),
        "wr": a["L0_ffn_W_router"], "br": row(a["L0_ffn_b_router"]),
        "w1": a["L0_ffn_W1"], "b1": a["L0_ffn_b1"].reshape(NE, FC, P).transpose(2, 0, 1), "w2": a["L0_ffn_W2"], "b2": row(a["L0_ffn_b2"]),
        **constants(),
    }
    arrays = {k: np.ascontiguousarray(v) for k, v in arrays.items()}
    nc = bacc.Bacc("TRN2", target_bir_lowering=False, num_devices=1)
    t = {k: nc.dram_tensor("in_" + k, v.shape, mybir.dt.from_np(v.dtype), kind="ExternalInput").ap()
         for k, v in arrays.items()}
    t["out"] = nc.dram_tensor("out", [TOK + P, D], F32, kind="ExternalOutput").ap()
    build(nc, t)
    r = run_bass_kernel_spmd(nc, [{"in_" + k: v for k, v in arrays.items()}], core_ids=[0])
    return r.results[0]["out"][:TOK].reshape(NB, S, D)
```
